# Optimizing a Trainium2 kernel written in Bass

```python
import numpy as np
import jax
import jax.numpy as jnp

def _softmax(x, axis=-1):
    return jax.nn.softmax(x, axis=axis)

def _gelu(x):
    return jax.nn.gelu(x, approximate=True)

def _silu(x):
    return jax.nn.silu(x)

def _sigmoid(x):
    return jax.nn.sigmoid(x)

def _layernorm(x, axis=-1, eps=1e-05):
    m = jnp.mean(x, axis=axis, keepdims=True)
    v = jnp.var(x, axis=axis, keepdims=True)
    return (x - m) / jnp.sqrt(v + eps)

def _scatter_add(tgt, idx, src, axis=0):
    return tgt.at[idx].add(src)

def _segment_sum(src, seg, n):
    return jax.ops.segment_sum(src, seg, n)
kernel_name = 'mk_seq_preln_d2_jaxref_r8_991cf0'

def setup_inputs(seed: int=0):
    np.random.seed(seed)
    _w = jnp.asarray

    def _L0_attn_setup():
        import jax, jax.numpy as jnp
        import numpy as np
        from jax import lax
        B = 2
        L = 256
        D_MODEL = 128
        D_STATE = 16
        D_CONV = 4
        D_INNER = 2 * D_MODEL
        CHUNK = 32

        def _selective_scan(u, delta, A, Bm, Cm, Dp):
            Bsz, Ln, d_inner = u.shape
            d_state = A.shape[1]
            nchunks = Ln // CHUNK
            dA = jnp.minimum(jnp.exp(delta[..., None] * A[None, None]), 1.0)
            dBu = delta[..., None] * Bm[:, :, None, :] * u[..., None]
            dA_c = dA.reshape(Bsz, nchunks, CHUNK, d_inner, d_state).transpose(1, 0, 2, 3, 4)
            dBu_c = dBu.reshape(Bsz, nchunks, CHUNK, d_inner, d_state).transpose(1, 0, 2, 3, 4)
            C_c = Cm.reshape(Bsz, nchunks, CHUNK, d_state).transpose(1, 0, 2, 3)

            def step(h, inp):
                dAk, dBuk, Ck = inp
                log_dA = jnp.log(jnp.maximum(dAk, 1e-08))
                cum = jnp.cumsum(log_dA, axis=1)
                cum_dA = jnp.exp(jnp.minimum(cum, 20.0))
                inv = jnp.exp(-jnp.minimum(jnp.maximum(cum, -20.0), 20.0))
                states = cum_dA * (h[:, None] + jnp.cumsum(dBuk * inv, axis=1))
                yk = (states * Ck[:, :, None, :]).sum(-1)
                return (states[:, -1], yk)
            h0 = jnp.zeros((Bsz, d_inner, d_state), u.dtype)
            _, ys = lax.scan(step, h0, (dA_c, dBu_c, C_c))
            y = ys.transpose(1, 0, 2, 3).reshape(Bsz, Ln, d_inner)
            return y + u * Dp[None, None, :]
        key = jax.random.key(seed)
        ks = jax.random.split(key, 8)
        s = 0.02
        x = jax.random.normal(ks[0], (B, L, D_MODEL), jnp.float32)
        in_proj_w = jax.random.normal(ks[1], (D_MODEL, 2 * D_INNER), jnp.float32) * s
        conv_w = jax.random.normal(ks[2], (D_INNER, 1, D_CONV), jnp.float32) * s
        conv_b = jnp.zeros((D_INNER,), jnp.float32)
        x_proj_w = jax.random.normal(ks[3], (D_INNER, 2 * D_STATE + 1), jnp.float32) * s
        dt_w = jax.random.uniform(ks[4], (1, D_INNER), jnp.float32, -0.02, 0.02)
        dt = jnp.exp(jax.random.uniform(ks[5], (D_INNER,), jnp.float32) * (np.float32(np.log(0.1)) - np.float32(np.log(0.001))) + np.float32(np.log(0.001)))
        dt_b = dt + jnp.log(-jnp.expm1(-dt))
        A_log = jnp.log(jnp.tile(jnp.arange(1, D_STATE + 1, dtype=jnp.float32)[None, :], (D_INNER, 1)))
        D_param = jnp.ones((D_INNER,), jnp.float32)
        out_proj_w = jax.random.normal(ks[6], (D_INNER, D_MODEL), jnp.float32) * s
        return {'x': x, 'in_proj_w': in_proj_w, 'conv_w': conv_w, 'conv_b': conv_b, 'x_proj_w': x_proj_w, 'dt_w': dt_w, 'dt_b': dt_b, 'A_log': A_log, 'D_param': D_param, 'out_proj_w': out_proj_w}
    _L0_attn_in = _L0_attn_setup()

    def _L0_ffn_setup():
        import jax, jax.numpy as jnp
        import numpy as np
        D_MODEL = 128
        N_EXPERTS = 8
        TOP_K = 2
        HIDDEN = 4 * D_MODEL
        key = jax.random.key(seed)
        ks = jax.random.split(key, 6)
        B, S = (2, 256)
        x = jax.random.normal(ks[0], (B, S, D_MODEL), dtype=jnp.float32)
        shared_w1 = jax.random.normal(ks[1], (HIDDEN, D_MODEL), dtype=jnp.float32) * 0.02
        shared_w2 = jax.random.normal(ks[2], (D_MODEL, HIDDEN), dtype=jnp.float32) * 0.02
        experts_w1 = jax.random.normal(ks[3], (N_EXPERTS, HIDDEN, D_MODEL), dtype=jnp.float32) * 0.02
        experts_w2 = jax.random.normal(ks[4], (N_EXPERTS, D_MODEL, HIDDEN), dtype=jnp.float32) * 0.02
        gate_w = jax.random.normal(ks[5], (N_EXPERTS, D_MODEL), dtype=jnp.float32) * 0.02
        return {'x': x, 'shared_w1': shared_w1, 'shared_w2': shared_w2, 'experts_w1': experts_w1, 'experts_w2': experts_w2, 'gate_w': gate_w}
    _L0_ffn_in = _L0_ffn_setup()

    def _L1_attn_setup():
        import jax, jax.numpy as jnp
        import numpy as np
        from math import sqrt
        D, H, B, L = (128, 16, 2, 256)
        DK = D // H

        def linear(x, w, b):
            return x @ w.T + b

        def conv1d(x, w, b, padding, groups=1):
            y = jax.lax.conv_general_dilated(x, w, window_strides=(1,), padding=(padding,), dimension_numbers=('NCH', 'OIH', 'NCH'), feature_group_count=groups)
            return y + b[None, :, None]
        key = jax.random.key(seed)
        ks = jax.random.split(key, 26)

        def n(k, shape, s=0.02):
            return jax.random.normal(k, shape, jnp.float32) * s
        return {'x': jax.random.normal(ks[0], (B, L, D), jnp.float32), 'Wq_w': n(ks[1], (D, D)), 'Wq_b': n(ks[2], (D,)), 'Wk_w': n(ks[3], (D, D)), 'Wk_b': n(ks[4], (D,)), 'Wv_w': n(ks[5], (D, D)), 'Wv_b': n(ks[6], (D,)), 'convq_w': n(ks[7], (D, D, 3)), 'convq_b': n(ks[8], (D,)), 'convk_w': n(ks[9], (D, D, 3)), 'convk_b': n(ks[10], (D,)), 'qproj_w': n(ks[11], (D, 2 * D)), 'qproj_b': n(ks[12], (D,)), 'kproj_w': n(ks[13], (D, 2 * D)), 'kproj_b': n(ks[14], (D,)), 'tau1_w': n(ks[15], (2 * D, 1, 3)), 'tau1_b': n(ks[16], (2 * D,)), 'tau2_w': n(ks[17], (H, 2 * D, 1)), 'tau2_b': n(ks[18], (H,)), 'del1_w': n(ks[19], (2 * D, 1, 3)), 'del1_b': n(ks[20], (2 * D,)), 'del2_w': n(ks[21], (H, 2 * D, 1)), 'del2_b': n(ks[22], (H,)), 'out_w': n(ks[23], (D, D)), 'out_b': n(ks[24], (D,))}
    _L1_attn_in = _L1_attn_setup()

    def _L1_ffn_setup():
        import jax, jax.numpy as jnp
        import numpy as np
        HIDDEN = 128
        NUM_EXPERTS = 8
        TOP_K = 2
        B, S = (2, 256)
        key = jax.random.key(seed)
        k1, k2, k3, k4, k5 = jax.random.split(key, 5)
        d, dff, E = (HIDDEN, 4 * HIDDEN, NUM_EXPERTS)
        x = jax.random.normal(k1, (B, S, d), dtype=jnp.float32)
        W1 = jax.random.normal(k2, (E, d, dff), dtype=jnp.float32) * (1.0 / np.sqrt(d))
        b1 = jax.random.normal(k3, (E, dff), dtype=jnp.float32) * 0.01
        W2 = jax.random.normal(k4, (E, dff, d), dtype=jnp.float32) * (1.0 / np.sqrt(dff))
        b2 = jax.random.normal(k5, (E, d), dtype=jnp.float32) * 0.01
        return {'x': x, 'W1': W1, 'b1': b1, 'W2': W2, 'b2': b2}
    _L1_ffn_in = _L1_ffn_setup()
    _d = {'L0_attn_x': _L0_attn_in['x'], 'L0_attn_in_proj_w': _L0_attn_in['in_proj_w'], 'L0_attn_conv_w': _L0_attn_in['conv_w'], 'L0_attn_conv_b': _L0_attn_in['conv_b'], 'L0_attn_x_proj_w': _L0_attn_in['x_proj_w'], 'L0_attn_dt_w': _L0_attn_in['dt_w'], 'L0_attn_dt_b': _L0_attn_in['dt_b'], 'L0_attn_A_log': _L0_attn_in['A_log'], 'L0_attn_D_param': _L0_attn_in['D_param'], 'L0_attn_out_proj_w': _L0_attn_in['out_proj_w'], 'L0_ffn_shared_w1': _L0_ffn_in['shared_w1'], 'L0_ffn_shared_w2': _L0_ffn_in['shared_w2'], 'L0_ffn_experts_w1': _L0_ffn_in['experts_w1'], 'L0_ffn_experts_w2': _L0_ffn_in['experts_w2'], 'L0_ffn_gate_w': _L0_ffn_in['gate_w'], 'L1_attn_Wq_w': _L1_attn_in['Wq_w'], 'L1_attn_Wq_b': _L1_attn_in['Wq_b'], 'L1_attn_Wk_w': _L1_attn_in['Wk_w'], 'L1_attn_Wk_b': _L1_attn_in['Wk_b'], 'L1_attn_Wv_w': _L1_attn_in['Wv_w'], 'L1_attn_Wv_b': _L1_attn_in['Wv_b'], 'L1_attn_convq_w': _L1_attn_in['convq_w'], 'L1_attn_convq_b': _L1_attn_in['convq_b'], 'L1_attn_convk_w': _L1_attn_in['convk_w'], 'L1_attn_convk_b': _L1_attn_in['convk_b'], 'L1_attn_qproj_w': _L1_attn_in['qproj_w'], 'L1_attn_qproj_b': _L1_attn_in['qproj_b'], 'L1_attn_kproj_w': _L1_attn_in['kproj_w'], 'L1_attn_kproj_b': _L1_attn_in['kproj_b'], 'L1_attn_tau1_w': _L1_attn_in['tau1_w'], 'L1_attn_tau1_b': _L1_attn_in['tau1_b'], 'L1_attn_tau2_w': _L1_attn_in['tau2_w'], 'L1_attn_tau2_b': _L1_attn_in['tau2_b'], 'L1_attn_del1_w': _L1_attn_in['del1_w'], 'L1_attn_del1_b': _L1_attn_in['del1_b'], 'L1_attn_del2_w': _L1_attn_in['del2_w'], 'L1_attn_del2_b': _L1_attn_in['del2_b'], 'L1_attn_out_w': _L1_attn_in['out_w'], 'L1_attn_out_b': _L1_attn_in['out_b'], 'L1_ffn_W1': _L1_ffn_in['W1'], 'L1_ffn_b1': _L1_ffn_in['b1'], 'L1_ffn_W2': _L1_ffn_in['W2'], 'L1_ffn_b2': _L1_ffn_in['b2']}
    _x0 = _d['L0_attn_x']
    _d['L0_attn_x'] = jax.random.normal(jax.random.fold_in(jax.random.key(seed), 1), (1, 2048, 128), dtype=_x0.dtype)
    del _x0
    return _d

def reference(L0_attn_x, L0_attn_in_proj_w, L0_attn_conv_w, L0_attn_conv_b, L0_attn_x_proj_w, L0_attn_dt_w, L0_attn_dt_b, L0_attn_A_log, L0_attn_D_param, L0_attn_out_proj_w, L0_ffn_shared_w1, L0_ffn_shared_w2, L0_ffn_experts_w1, L0_ffn_experts_w2, L0_ffn_gate_w, L1_attn_Wq_w, L1_attn_Wq_b, L1_attn_Wk_w, L1_attn_Wk_b, L1_attn_Wv_w, L1_attn_Wv_b, L1_attn_convq_w, L1_attn_convq_b, L1_attn_convk_w, L1_attn_convk_b, L1_attn_qproj_w, L1_attn_qproj_b, L1_attn_kproj_w, L1_attn_kproj_b, L1_attn_tau1_w, L1_attn_tau1_b, L1_attn_tau2_w, L1_attn_tau2_b, L1_attn_del1_w, L1_attn_del1_b, L1_attn_del2_w, L1_attn_del2_b, L1_attn_out_w, L1_attn_out_b, L1_ffn_W1, L1_ffn_b1, L1_ffn_W2, L1_ffn_b2):

    def _L0_attn_ref(x, in_proj_w, conv_w, conv_b, x_proj_w, dt_w, dt_b, A_log, D_param, out_proj_w):
        import jax, jax.numpy as jnp
        import numpy as np
        from jax import lax
        B = 2
        L = 256
        D_MODEL = 128
        D_STATE = 16
        D_CONV = 4
        D_INNER = 2 * D_MODEL
        CHUNK = 32

        def _selective_scan(u, delta, A, Bm, Cm, Dp):
            Bsz, Ln, d_inner = u.shape
            d_state = A.shape[1]
            nchunks = Ln // CHUNK
            dA = jnp.minimum(jnp.exp(delta[..., None] * A[None, None]), 1.0)
            dBu = delta[..., None] * Bm[:, :, None, :] * u[..., None]
            dA_c = dA.reshape(Bsz, nchunks, CHUNK, d_inner, d_state).transpose(1, 0, 2, 3, 4)
            dBu_c = dBu.reshape(Bsz, nchunks, CHUNK, d_inner, d_state).transpose(1, 0, 2, 3, 4)
            C_c = Cm.reshape(Bsz, nchunks, CHUNK, d_state).transpose(1, 0, 2, 3)

            def step(h, inp):
                dAk, dBuk, Ck = inp
                log_dA = jnp.log(jnp.maximum(dAk, 1e-08))
                cum = jnp.cumsum(log_dA, axis=1)
                cum_dA = jnp.exp(jnp.minimum(cum, 20.0))
                inv = jnp.exp(-jnp.minimum(jnp.maximum(cum, -20.0), 20.0))
                states = cum_dA * (h[:, None] + jnp.cumsum(dBuk * inv, axis=1))
                yk = (states * Ck[:, :, None, :]).sum(-1)
                return (states[:, -1], yk)
            h0 = jnp.zeros((Bsz, d_inner, d_state), u.dtype)
            _, ys = lax.scan(step, h0, (dA_c, dBu_c, C_c))
            y = ys.transpose(1, 0, 2, 3).reshape(Bsz, Ln, d_inner)
            return y + u * Dp[None, None, :]
        d_state = (x_proj_w.shape[1] - 1) // 2
        xz = x @ in_proj_w
        x_in, z = jnp.split(xz, 2, axis=-1)
        xc = x_in.transpose(0, 2, 1)
        xc = lax.conv_general_dilated(xc, conv_w, (1,), [(D_CONV - 1, 0)], feature_group_count=conv_w.shape[0], dimension_numbers=('NCH', 'OIH', 'NCH')) + conv_b[None, :, None]
        xc = jax.nn.silu(xc.transpose(0, 2, 1))
        ssm_out = xc @ x_proj_w
        B_p = ssm_out[..., :d_state]
        C_p = ssm_out[..., d_state:2 * d_state]
        dt = jax.nn.softplus(ssm_out[..., -1:] @ dt_w + dt_b)
        A = -jnp.exp(A_log)
        y = _selective_scan(xc, dt, A, B_p, C_p, D_param)
        return y * jax.nn.silu(z) @ out_proj_w

    def _L0_ffn_ref(x, shared_w1, shared_w2, experts_w1, experts_w2, gate_w):
        import jax, jax.numpy as jnp
        import numpy as np
        D_MODEL = 128
        N_EXPERTS = 8
        TOP_K = 2
        HIDDEN = 4 * D_MODEL
        B, S, D = x.shape
        T = B * S
        x_flat = x.reshape(T, D)
        shared = jnp.einsum('td,dh->th', x_flat, shared_w1.T)
        shared = jnp.einsum('th,hd->td', jax.nn.silu(shared), shared_w2.T)
        gate_logits = x_flat @ gate_w.T
        top_k_gates, top_k_idx = jax.lax.top_k(gate_logits, TOP_K)
        top_k_gates = jax.nn.softmax(top_k_gates, axis=1)
        gates = jnp.zeros((T, N_EXPERTS), dtype=x.dtype)
        gates = gates.at[jnp.arange(T)[:, None], top_k_idx].set(top_k_gates)
        h = jnp.einsum('td,ehd->teh', x_flat, experts_w1)
        expert_out = jnp.einsum('teh,edh->ted', jax.nn.silu(h), experts_w2)
        selected = jnp.einsum('ted,te->td', expert_out, gates)
        return (shared + selected).reshape(B, S, D)

    def _L1_attn_ref(x, Wq_w, Wq_b, Wk_w, Wk_b, Wv_w, Wv_b, convq_w, convq_b, convk_w, convk_b, qproj_w, qproj_b, kproj_w, kproj_b, tau1_w, tau1_b, tau2_w, tau2_b, del1_w, del1_b, del2_w, del2_b, out_w, out_b):
        import jax, jax.numpy as jnp
        import numpy as np
        from math import sqrt
        D, H, B, L = (128, 16, 2, 256)
        DK = D // H

        def linear(x, w, b):
            return x @ w.T + b

        def conv1d(x, w, b, padding, groups=1):
            y = jax.lax.conv_general_dilated(x, w, window_strides=(1,), padding=(padding,), dimension_numbers=('NCH', 'OIH', 'NCH'), feature_group_count=groups)
            return y + b[None, :, None]
        b_, l_, _ = x.shape
        q_in = linear(x, Wq_w, Wq_b).transpose(0, 2, 1)
        Q3 = conv1d(q_in, convq_w, convq_b, (1, 1))
        Q_cat = jnp.concatenate([q_in, Q3], axis=1).transpose(0, 2, 1)
        Q = linear(Q_cat, qproj_w, qproj_b).reshape(b_, l_, H, DK).transpose(0, 2, 1, 3)
        k_in = linear(x, Wk_w, Wk_b).transpose(0, 2, 1)
        K3 = conv1d(k_in, convk_w, convk_b, (1, 1))
        K_cat = jnp.concatenate([k_in, K3], axis=1).transpose(0, 2, 1)
        K = linear(K_cat, kproj_w, kproj_b).reshape(b_, l_, H, DK).transpose(0, 2, 1, 3)
        V = linear(x, Wv_w, Wv_b).reshape(b_, l_, H, DK).transpose(0, 2, 1, 3)
        x_conv = x.transpose(0, 2, 1)
        tau = jax.nn.sigmoid(conv1d(jax.nn.gelu(conv1d(x_conv, tau1_w, tau1_b, (1, 1), groups=D), approximate=False), tau2_w, tau2_b, (0, 0)))
        delta = jax.nn.sigmoid(conv1d(jax.nn.gelu(conv1d(x_conv, del1_w, del1_b, (1, 1), groups=D), approximate=False), del2_w, del2_b, (0, 0)))
        scores = jnp.einsum('bhqd,bhkd->bhqk', Q, K) / sqrt(DK)
        scores = scores * tau[..., None] + delta[:, :, None, :]
        attn = jax.nn.softmax(scores, axis=-1)
        out = jnp.einsum('bhqk,bhkd->bhqd', attn, V)
        out = out.transpose(0, 2, 1, 3).reshape(b_, l_, D)
        return linear(out, out_w, out_b)

    def _L1_ffn_ref(x, W1, b1, W2, b2):
        import jax, jax.numpy as jnp
        import numpy as np
        HIDDEN = 128
        NUM_EXPERTS = 8
        TOP_K = 2
        B, S = (2, 256)
        Bm, Sm, d = x.shape
        E = W1.shape[0]
        x_flat = x.reshape(-1, d)
        h = jnp.mod(x_flat[:, :TOP_K].sum(axis=1).astype(jnp.int32), E)
        sel = jnp.stack([h, jnp.mod(h + 1, E)], axis=1)

        def step(acc, params):
            e, W1e, b1e, W2e, b2e = params
            w = jnp.any(sel == e, axis=1).astype(x.dtype) / TOP_K
            y = jnp.maximum(x_flat @ W1e + b1e, 0.0) @ W2e + b2e
            return (acc + w[:, None] * y, None)
        init = jnp.zeros_like(x_flat)
        out_flat, _ = jax.lax.scan(step, init, (jnp.arange(E), W1, b1, W2, b2))
        return out_flat.reshape(Bm, Sm, d)
    x = L0_attn_x
    x = x + _L0_attn_ref(_layernorm(x, axis=-1), L0_attn_in_proj_w, L0_attn_conv_w, L0_attn_conv_b, L0_attn_x_proj_w, L0_attn_dt_w, L0_attn_dt_b, L0_attn_A_log, L0_attn_D_param, L0_attn_out_proj_w)
    x = x + _L0_ffn_ref(_layernorm(x, axis=-1), L0_ffn_shared_w1, L0_ffn_shared_w2, L0_ffn_experts_w1, L0_ffn_experts_w2, L0_ffn_gate_w)
    x = x + _L1_attn_ref(_layernorm(x, axis=-1), L1_attn_Wq_w, L1_attn_Wq_b, L1_attn_Wk_w, L1_attn_Wk_b, L1_attn_Wv_w, L1_attn_Wv_b, L1_attn_convq_w, L1_attn_convq_b, L1_attn_convk_w, L1_attn_convk_b, L1_attn_qproj_w, L1_attn_qproj_b, L1_attn_kproj_w, L1_attn_kproj_b, L1_attn_tau1_w, L1_attn_tau1_b, L1_attn_tau2_w, L1_attn_tau2_b, L1_attn_del1_w, L1_attn_del1_b, L1_attn_del2_w, L1_attn_del2_b, L1_attn_out_w, L1_attn_out_b)
    x = x + _L1_ffn_ref(_layernorm(x, axis=-1), L1_ffn_W1, L1_ffn_b1, L1_ffn_W2, L1_ffn_b2)
    return x

_drawn_inputs = setup_inputs


def setup_inputs(seed=0):
    import zlib

    import numpy as np

    out = dict(_drawn_inputs(seed))
    spreads = {'L0_attn_conv_b': (0.0, 0.711), 'L0_attn_D_param': (1.0, 0.6)}
    factors = {'L0_attn_in_proj_w': 4.396,
     'L0_attn_conv_w': 8.0,
     'L0_attn_x_proj_w': 8.0,
     'L0_attn_dt_w': 8.0,
     'L0_attn_dt_b': 8.0,
     'L0_attn_A_log': 8.0,
     'L0_attn_out_proj_w': 5.458,
     'L1_attn_Wq_w': 8.0,
     'L1_attn_Wq_b': 8.0,
     'L1_attn_Wk_w': 8.0,
     'L1_attn_Wk_b': 8.0,
     'L1_attn_Wv_w': 7.25,
     'L1_attn_Wv_b': 6.255,
     'L1_attn_convq_w': 8.0,
     'L1_attn_convq_b': 8.0,
     'L1_attn_convk_w': 8.0,
     'L1_attn_convk_b': 8.0,
     'L1_attn_qproj_w': 8.0,
     'L1_attn_qproj_b': 8.0,
     'L1_attn_kproj_w': 8.0,
     'L1_attn_kproj_b': 8.0,
     'L1_attn_tau1_w': 8.0,
     'L1_attn_tau1_b': 8.0,
     'L1_attn_tau2_w': 8.0,
     'L1_attn_tau2_b': 8.0,
     'L1_attn_del1_w': 8.0,
     'L1_attn_del1_b': 8.0,
     'L1_attn_del2_w': 8.0,
     'L1_attn_del2_b': 8.0,
     'L1_attn_out_w': 4.142,
     'L1_ffn_b1': 8.0,
     'L1_ffn_b2': 8.0}
    for name, (base, spread) in spreads.items():
        noise = np.random.default_rng([zlib.crc32(name.encode()), seed]).standard_normal(out[name].shape)
        drawn = base * np.exp(spread * noise) if base else spread * noise
        out[name] = jnp.asarray(drawn.astype(out[name].dtype))
    for name, factor in factors.items():
        out[name] = (out[name] * factor).astype(out[name].dtype)
    return out
```

```python
from contextlib import ExitStack

import concourse.bass as bass
import numpy as np
from concourse import mybir

ALU = mybir.AluOpType
ACT = mybir.ActivationFunctionType
AX = mybir.AxisListType
F32 = mybir.dt.float32
BF16 = mybir.dt.bfloat16

T = 2048
NB = T // 128
NE = 8
NH = 16
TQ = 1024
E20 = float(np.float32(np.exp(20.0)))
LOG1P = [0.9999999992732804, -0.49999981737027194, 0.3333256943206084, -0.24987395019953507,
         0.1989154870228832, -0.16108664975266748, 0.12425163151193669, -0.08253601410389311,
         0.04155808633524785, -0.013445002542276745, 0.002037716592261226]


class Lane:

    def __init__(self, name, sem):
        self.name, self.sem, self.count, self.seen, self.items = name, sem, 0, {}, []

    def wait(self, *marks):
        for m in marks:
            if m is None:
                continue
            if isinstance(m, list):
                self.wait(*m)
                continue
            sem, value = m
            if self.seen.get(sem.name, 0) < value:
                self.seen[sem.name] = value
                self.items.append(lambda e, s=sem, v=value: e.wait_ge(s, v))

    def do(self, fn, *marks):
        self.wait(*marks)
        self.count += 1
        self.items.append(lambda e, s=self.sem: fn(e).then_inc(s, 1))
        return (self.sem, self.count)

    def quiet(self, fn, *marks):
        self.wait(*marks)
        self.items.append(lambda e: fn(e))

    def play(self, e):
        for item in self.items:
            item(e)


class Loads:

    def __init__(self, sem):
        self.sem, self.count = sem, 0

    def start(self, lane, out, in_, *marks):
        lane.wait(*marks)
        self.count += 16
        lane.items.append(lambda e: e.dma_start(out, in_).then_inc(self.sem, 16))

    def mark(self):
        return (self.sem, self.count)


def build(nc, A, out):
    with ExitStack() as ctx:
        def sem(name):
            return ctx.enter_context(nc.semaphore(name))

        pe, act, dve, pool, sp = (Lane(n, sem("s_" + n)) for n in ("pe", "act", "dve", "pool", "sp"))
        lanes = (pe, act, dve, pool, sp)
        used = [0]

        def sb(name, shape, dt=F32, stack=ctx):
            return stack.enter_context(nc.sbuf_tensor(name, shape, dt))

        def loads(name):
            return Loads(sem(name))

        def scratch(name, shape, dt):
            return nc.dram_tensor(name, shape, dt, kind="Internal").ap()

        PS = ctx.enter_context(nc.psum_tensor("PS", [128, 8, 512], F32))

        def bank(i, n=1):
            return PS[:, i, :] if n == 1 else PS[:, i:i + n, :].rearrange("p a b -> p (a b)")

        def meet():
            marks = [(x.sem, x.count) for x in lanes if x.count]
            for x in lanes:
                x.wait(*marks)

        x_tok = sb("x_tok", [128, NB, 128])
        xnT = sb("xnT", [128, T + 2])
        XN = xnT[:, 1:T + 1]
        ident = sb("ident", [128, 128])
        identb = sb("identb", [128, 128], BF16)
        sel = sb("sel", [96, 32, 128], BF16)
        cst = sb("cst", [128, 4])
        st6 = sb("st6", [128, NB, 6])
        mv = sb("mv", [128, NB, 2])
        rstd = sb("rstd", [128, NB])
        mhalf = sb("mhalf", [128, NB])

        d_x = loads("d_x")
        d_a = loads("d_a")
        d_f = loads("d_f")
        xv = A["L0_attn_x"].rearrange("o (b p) d -> p (o b) d", p=128)
        d_x.start(sp, x_tok[:, :, :], xv)

        c0 = pool.do(lambda e: e.memset(ident[:, :], 0.0))
        c1 = pool.do(lambda e: e.affine_select(out=ident[:, :], in_=ident[:, :], compare_op=ALU.not_equal, fill=1.0,
                                               base=0, pattern=[[-1, 128]], channel_multiplier=1), c0)
        s0 = pool.do(lambda e: e.memset(sel[:, :, :], 0.0))
        for k in range(3):
            s0 = pool.do(lambda e, k=k: e.affine_select(
                out=sel[:, :, :], in_=sel[:, :, :], compare_op=ALU.not_equal, fill=1.0,
                base=-32 * k, pattern=[[-1, 32], [0, 128]], channel_multiplier=1), s0)
        c_sel = s0
        c2 = pool.do(lambda e: e.memset(mhalf[:, :], -0.5))
        c3 = dve.do(lambda e: e.memset(xnT[:, 0:1], 0.0))
        c4 = dve.do(lambda e: e.memset(xnT[:, T + 1:T + 2], 0.0))
        c_const = [c1, c_sel, c2, c3, c4]

        def split3(lane_src, src, outs, r1, r2, *marks):
            m = dve.do(lambda e: e.tensor_copy(outs[0], src), *marks)
            m1 = dve.do(lambda e: e.tensor_tensor(r1, src, outs[0], ALU.subtract), m)
            m = dve.do(lambda e: e.tensor_copy(outs[1], r1), m1)
            m2 = dve.do(lambda e: e.tensor_tensor(r2, r1, outs[1], ALU.subtract), m)
            return dve.do(lambda e: e.tensor_copy(outs[2], r2), m2)

        def layernorm(xn, after, bank0=0, keep=None):
            m = None
            for b in range(NB):
                m = dve.do(lambda e, b=b: e.bn_stats(st6[:, b, :], x_tok[:, b, :]), *after)
            ms = [dve.do(lambda e, b=b: e.bn_aggr(mv[:, b, :], st6[:, b, :]), m) for b in range(NB)]
            m = dve.do(lambda e: e.tensor_scalar(rstd[:, :], mv[:, :, 1], 1e-5, None, ALU.add), ms[-1])
            m = pool.do(lambda e: e.tensor_tensor(rstd[:, :], rstd[:, :], mhalf[:, :], ALU.pow), m, c2)
            done = []
            free = [None, None]
            for q in range(4):
                for b in range(4 * q, 4 * q + 4):
                    n = dve.do(lambda e, b=b: e.tensor_scalar(xn[:, b, :], x_tok[:, b, :], mv[:, b, 0:1],
                                                              rstd[:, b:b + 1], ALU.subtract, ALU.mult), m)
                for b in range(4 * q, 4 * q + 4):
                    t = pe.do(lambda e, b=b, q=q: e.transpose(bank(bank0 + q % 2)[:, (b % 4) * 128:(b % 4 + 1) * 128],
                                                              xn[:, b, :], ident[:, :]), n, free[q % 2], c1)
                free[q % 2] = act.do(lambda e, q=q: e.activation(XN[:, 512 * q:512 * q + 512], bank(bank0 + q % 2),
                                                                 ACT.Copy), t)
                done.append(free[q % 2])
            return done

        def mm(o, l, r, start, stop, *marks, sig=False):
            f = pe.do if sig else pe.quiet
            return f(lambda e: e.matmul(o, l, r, start=start, stop=stop), *marks)

        def stage1(ph):
            def sa(name, shape, dt=F32):
                return sb(name, shape, dt, ph)

            w_in = sa("w_in", [128, 512])
            w_cv = sa("w_cv", [128, 2, 4])
            w_cb = sa("w_cb", [128, 2])
            w_xp = sa("w_xp", [128, 2, 33])
            w_dt = sa("w_dt", [33, 256])
            w_db = sa("w_db", [128, 2])
            w_al = sa("w_al", [128, 2, 16])
            w_D = sa("w_D", [128, 2])
            w_out = sa("w_out", [128, 2, 128])
            Am = sa("Am", [128, 32])
            u = sa("u", [128, 2, T])
            zs = sa("zs", [128, 2, T])
            dl = sa("dl", [128, 2, T])
            du = sa("du", [128, 2, T])
            ssm3 = sa("ssm3", [96, T], BF16)
            hl = sa("hl", [128, 32])
            arena = sa("arena", [128, 20480])
            d_a.start(sp, w_in[:, :], A["L0_attn_in_proj_w"])
            d_a.start(sp, w_cv[:, :, :], A["L0_attn_conv_w"].rearrange("(g p) o k -> p g (o k)", p=128))
            d_a.start(sp, w_cb[:, :], A["L0_attn_conv_b"])
            d_a.start(sp, w_xp[:, :, :], A["L0_attn_x_proj_w"].rearrange("(g p) n -> p g n", p=128))
            d_a.start(sp, w_dt[32:33, :], A["L0_attn_dt_w"])
            d_a.start(sp, w_db[:, :], A["L0_attn_dt_b"])
            d_a.start(sp, w_al[:, :, :], A["L0_attn_A_log"].rearrange("(g p) n -> p g n", p=128))
            d_a.start(sp, w_D[:, :], A["L0_attn_D_param"])
            d_a.start(sp, w_out[:, :, :], A["L0_attn_out_proj_w"].rearrange("(g p) n -> p g n", p=128))
            wa = d_a.mark()

            xn = arena[:, 0:2048].rearrange("p (b d) -> p b d", b=NB)
            ln = layernorm(xn, [d_x.mark()])
            xin = arena[:, 2048:2048 + 2 * (T + 3)].rearrange("p (g t) -> p g t", g=2)
            cv = arena[:, 8192:8192 + 2 * T].rearrange("p (g t) -> p g t", g=2)
            z0 = dve.do(lambda e: e.memset(xin[:, :, 0:3], 0.0))
            mA = act.do(lambda e: e.activation(Am[:, :], w_al[:, :, :].rearrange("p g n -> p (g n)"), ACT.Exp), wa)
            mA = act.do(lambda e: e.mul(Am[:, :], Am[:, :], -1.0), mA)
            free = [None] * 8
            ev = {}
            for i, (m, q) in enumerate([(m, q) for m in range(4) for q in range(4)]):
                k = 2 + i % 4
                t = mm(bank(k), w_in[:, 128 * m:128 * m + 128], XN[:, 512 * q:512 * q + 512], True, True,
                       wa, ln[q], free[k], sig=True)
                if m < 2:
                    o = xin[:, m, 3 + 512 * q:3 + 512 * q + 512]
                    free[k] = act.do(lambda e, o=o, k=k: e.activation(o, bank(k), ACT.Copy), t)
                else:
                    o = zs[:, m - 2, 512 * q:512 * q + 512]
                    free[k] = act.do(lambda e, o=o, k=k: e.activation(o, bank(k), ACT.Silu), t)
                ev[m, q] = free[k]
            mu = []
            for g in range(2):
                m = dve.do(lambda e, g=g: e.tensor_scalar(cv[:, g, :], xin[:, g, 0:T], w_cv[:, g, 0:1],
                                                          w_cb[:, g:g + 1], ALU.mult, ALU.add), ev[g, 3], z0, wa)
                for j in range(1, 4):
                    m = dve.do(lambda e, g=g, j=j: e.scalar_tensor_tensor(
                        out=cv[:, g, :], in0=xin[:, g, j:j + T], scalar=w_cv[:, g, j:j + 1], in1=cv[:, g, :],
                        op0=ALU.mult, op1=ALU.add), m)
                mu.append(act.do(lambda e, g=g: e.activation(u[:, g, :], cv[:, g, :], ACT.Silu), m))
            row = arena[:, 2048:4096]
            ms = []
            for q in range(4):
                k = 2 + q
                for g in range(2):
                    t = mm(bank(k)[0:33, :], w_xp[:, g, :], u[:, g, 512 * q:512 * q + 512], g == 0, g == 1,
                           mu[g], free[k], sig=(g == 1))
                ms.append(act.do(lambda e, q=q, k=k: e.activation(row[0:33, 512 * q:512 * q + 512],
                                                                  bank(k)[0:33, :], ACT.Copy), t))
                free[k] = ms[-1]
            r1, r2 = arena[0:32, 4096:6144], arena[0:32, 8192:10240]
            m3 = split3(None, row[0:32, :], [ssm3[32 * k:32 * k + 32, :] for k in range(3)], r1, r2, ms[-1], mu[1])
            va, ya, pa = (arena[:, o:o + T] for o in (10240, 12288, 14336))
            mdu = []
            m = None
            for g in range(2):
                for q in range(4):
                    k = 2 + q
                    s = slice(512 * q, 512 * q + 512)
                    t = mm(bank(k), w_dt[32:33, 128 * g:128 * g + 128], row[32:33, s], True, True, ms[-1], free[k],
                           sig=True)
                    v1 = act.do(lambda e, s=s, k=k, g=g: e.activation(va[:, s], bank(k), ACT.Identity,
                                                                      bias=w_db[:, g:g + 1]), t, m, mu[1])
                    v2 = act.do(lambda e, s=s, k=k, g=g: e.activation(ya[:, s], bank(k), ACT.Abs,
                                                                      bias=w_db[:, g:g + 1]), t)
                    free[k] = v2
                v2 = act.do(lambda e: e.activation(ya[:, :], ya[:, :], ACT.Exp, scale=-1.0), v2)
                m = dve.do(lambda e: e.tensor_scalar(pa[:, :], ya[:, :], LOG1P[-1], None, ALU.mult), v2)
                for c in LOG1P[-2::-1]:
                    m = dve.do(lambda e, c=c: e.scalar_tensor_tensor(out=pa[:, :], in0=pa[:, :], scalar=c,
                                                                     in1=ya[:, :], op0=ALU.add, op1=ALU.mult), m)
                m = dve.do(lambda e, g=g: e.scalar_tensor_tensor(out=dl[:, g, :], in0=va[:, :], scalar=0.0,
                                                                 in1=pa[:, :], op0=ALU.max, op1=ALU.add), m)
                mdu.append(pool.do(lambda e, g=g: e.tensor_tensor(du[:, g, :], dl[:, g, :], u[:, g, :], ALU.mult),
                                   m, mu[g]))
            meet()
            NR = 3
            Bb = [arena[:, 1024 * i:1024 * i + TQ] for i in range(2)]
            Cb = [arena[:, 2048 + 1024 * i:2048 + 1024 * i + TQ] for i in range(2)]
            ab, rb, wb, pb = ([arena[:, 4096 + 1024 * (4 * i + j):4096 + 1024 * (4 * i + j) + TQ] for i in range(NR)]
                              for j in range(4))
            rz = [pool.do(lambda e, i=i: e.memset(rb[i], 0.0)) for i in range(NR)]
            freeB, freeC = [None, None], [None, None]
            fr = [dict(a=None, w=None, p=None, r=None) for _ in range(NR)]
            bfree = [None, None]
            yev = None
            hm = {}
            k = 0
            mfin = []
            for tc in range(T // TQ):
                ts = slice(TQ * tc, TQ * tc + TQ)
                ym = None
                for n in range(16):
                    i = n % 2
                    for w, (dst, row_, fz) in enumerate(((Bb, n, freeB), (Cb, 16 + n, freeC))):
                        b0 = 4 + 2 * w
                        for q in range(2):
                            t = mm(bank(b0 + q), sel[:, row_, :], ssm3[:, TQ * tc + 512 * q:TQ * tc + 512 * q + 512],
                                   True, True, bfree[w], m3, c_sel, sig=True)
                        bfree[w] = act.do(lambda e, d=dst[i], b0=b0: e.activation(d, bank(b0, 2), ACT.Copy), t, fz[i])
                    mB, mC = bfree
                    for g in range(2):
                        f = fr[k % NR]
                        a, r, w_, p = ab[k % NR], rb[k % NR], wb[k % NR], pb[k % NR]
                        c = 16 * g + n
                        m_a = act.do(lambda e, a=a, g=g, ts=ts, c=c: e.activation(a, dl[:, g, ts], ACT.Exp,
                                                                                  scale=Am[:, c:c + 1]), f["a"])
                        m_w = pool.do(lambda e, w_=w_, g=g, ts=ts, i=i: e.tensor_tensor(w_, du[:, g, ts], Bb[i],
                                                                                        ALU.mult), mB, f["w"])
                        m_a = dve.do(lambda e, a=a: e.tensor_scalar(a, a, 1.0, 1e-8, ALU.min, ALU.max), m_a)
                        m_r = act.do(lambda e, a=a, r=r: e.mul(r[:, 0:TQ:32], a[:, 0:TQ:32], E20), m_a, f["r"],
                                     rz[-1])
                        m_p = dve.do(lambda e, p=p, a=a, r=r: e.tensor_tensor_scan(
                            out=p, data0=a, data1=r, initial=0.0, op0=ALU.mult, op1=ALU.max), m_r, f["p"])
                        f["r"] = m_p
                        m_w = dve.do(lambda e, p=p, w_=w_: e.scalar_tensor_tensor(
                            out=w_, in0=p, scalar=1.0, in1=w_, op0=ALU.min, op1=ALU.mult), m_p, m_w)
                        freeB[i] = m_w
                        init = 0.0 if tc == 0 else hl[:, c:c + 1]
                        m_x = dve.do(lambda e, p=p, a=a, w_=w_, init=init: e.tensor_tensor_scan(
                            out=p, data0=a, data1=w_, initial=init, op0=ALU.mult, op1=ALU.add), m_w,
                            hm.get(c))
                        f["a"] = m_x
                        if tc < T // TQ - 1:
                            hm[c] = pool.do(lambda e, p=p, c=c: e.tensor_copy(hl[:, c:c + 1], p[:, TQ - 1:TQ]), m_x)
                        m_c = pool.do(lambda e, p=p, w_=w_, i=i: e.tensor_tensor(w_, p, Cb[i], ALU.mult), m_x, mC)
                        f["p"] = m_c
                        freeC[i] = m_c
                        for q in range(2):
                            t = mm(bank(2 * g + q), ident[:, :], w_[:, 512 * q:512 * q + 512], n == 0, n == 15,
                                   m_c, yev, sig=True)
                        f["w"] = t
                        k += 1
                for g in range(2):
                    m = dve.do(lambda e, g=g, ts=ts: e.scalar_tensor_tensor(
                        out=u[:, g, ts], in0=u[:, g, ts], scalar=w_D[:, g:g + 1], in1=bank(2 * g, 2),
                        op0=ALU.mult, op1=ALU.add), t)
                    yev = m
                    m = dve.do(lambda e, g=g, ts=ts: e.tensor_tensor(u[:, g, ts], u[:, g, ts], zs[:, g, ts],
                                                                     ALU.mult), m)
                mfin.append(m)
            meet()
            fz = [None, None]
            for q in range(4):
                b = 4 + q % 2
                for j in range(4):
                    tb = slice(512 * q + 128 * j, 512 * q + 128 * j + 128)
                    for g in range(2):
                        t = mm(bank(b)[:, 128 * j:128 * j + 128], u[:, g, tb], w_out[:, g, :], g == 0, g == 1,
                               fz[q % 2], sig=True)
                xs = x_tok[:, 4 * q:4 * q + 4, :].rearrange("p b d -> p (b d)")
                fz[q % 2] = dve.do(lambda e, xs=xs, b=b: e.tensor_tensor(xs, xs, bank(b), ALU.add), t)
            meet()

        def moe(W1, W2, gates3, xin_marks, nexp, h, hg, hid, bias, acc_extra, wmark):
            hb = [h[:, 0, :], h[:, 1, :], h[:, 2, :]]
            gb = [hg[:, 0, :], hg[:, 1, :], hg[:, 2, :]]
            fh, fg, fu, fG, fo = [None] * 3, [None] * 3, [None] * 3, [None] * 2, [None, None]
            ftr = [None]
            i = 0
            gi = 0
            for q in range(4):
                s = slice(512 * q, 512 * q + 512)
                ob = 6
                steps = [(e_, j) for e_ in range(nexp) for j in range(4)]
                pend = []
                gm = None
                for n, (e_, j) in enumerate(steps):
                    row_ = hid["rows"][e_]
                    if j == 0 and row_ is not None:
                        gbk = 3 + gi % 2
                        gm = mm(bank(gbk), sel[:, row_, :], gates3[:, s], True, True, fG[gi % 2], *xin_marks, sig=True)
                        gcur = gi % 2
                        gi += 1
                    k = i % 3
                    t = mm(bank(k), W1(e_, j), XN[:, s], True, True, fu[k], wmark, *xin_marks, sig=True)
                    m = act.do(lambda e, k=k, f=hid["f"], b=bias(e_, j): e.activation(hb[k], bank(k), f, bias=b),
                               t, fh[k])
                    fu[k] = m
                    if row_ is None:
                        src, owner = hb[k], fh
                    else:
                        m = dve.do(lambda e, k=k, gk=3 + gcur: e.tensor_tensor(gb[k], hb[k], bank(gk), ALU.mult),
                                   m, gm, fg[k])
                        fh[k] = m
                        fG[gcur] = m
                        src, owner = gb[k], fg
                    pend.append((n, e_, j, k, src, owner, m))
                    i += 1
                    if len(pend) > 2 or n == len(steps) - 1:
                        while len(pend) > (0 if n == len(steps) - 1 else 2):
                            n_, e2, j2, k2, src2, own2, m2 = pend.pop(0)
                            last = n_ == len(steps) - 1
                            t = mm(bank(ob), W2(e2, j2), src2, n_ == 0, last and acc_extra is None, m2, fo[0],
                                   sig=True)
                            own2[k2] = t
                            tl = t
                if acc_extra is not None:
                    tl = acc_extra(bank(ob), s)
                ev_ = act.do(lambda e: e.activation(hid["o"], bank(ob), ACT.Copy), tl, ftr[0])
                fo[0] = ev_
                for j in range(4):
                    tt = pe.do(lambda e, j=j: e.transpose(bank(7)[:, 128 * j:128 * j + 128],
                                                          hid["o"][:, 128 * j:128 * j + 128], ident[:, :]),
                               ev_, fo[1])
                ftr[0] = tt
                xs = x_tok[:, 4 * q:4 * q + 4, :].rearrange("p b d -> p (b d)")
                fo[1] = dve.do(lambda e, xs=xs: e.tensor_tensor(xs, xs, bank(7), ALU.add), tt)
                hid["done"](q, fo[1])

        def spread(G, gT, g3, r1, r2, zero, *marks):
            f = [None, None]
            ms = []
            for q in range(4):
                for b in range(4):
                    t = pe.do(lambda e, b=b, q=q: e.transpose(bank(q % 2)[0:8, 128 * b:128 * b + 128],
                                                              G[:, 4 * q + b, :], ident[:, :]), f[q % 2], *marks)
                f[q % 2] = act.do(lambda e, q=q: e.activation(gT[0:8, 512 * q:512 * q + 512], bank(q % 2)[0:8, :],
                                                              ACT.Copy), t)
                ms.append(f[q % 2])
            return split3(None, gT[0:8, :], [g3[32 * k:32 * k + 8, :] for k in range(3)], r1[0:8, :], r2[0:8, :],
                          ms[-1], zero)

        def stage2(ph):
            def sa(name, shape, dt=F32):
                return sb(name, shape, dt, ph)

            f_w1 = sa("f_w1", [128, 9, 512])
            f_w2 = sa("f_w2", [128, 9, 4, 128])
            f_g = sa("f_g", [128, 8])
            lg = sa("lg", [128, NB, 8])
            oh = sa("oh", [128, NB, 8])
            tmp = sa("tmp", [128, NB, 8])
            rank = sa("rank", [128, NB, 8])
            G = sa("G", [128, NB, 8])
            mx = sa("mx", [128, 4, NB])
            g3 = sa("g3", [96, T], BF16)
            ar = sa("ar", [128, 10240])
            d_f.start(sp, f_w1[:, 0, :], A["L0_ffn_shared_w1"])
            d_f.start(sp, f_w1[:, 1:9, :], A["L0_ffn_experts_w1"].rearrange("e d h -> d e h"))
            d_f.start(act, f_w2[:, 0, :, :], A["L0_ffn_shared_w2"].rearrange("(k p) d -> p k d", p=128))
            for x in range(8):
                d_f.start(act, f_w2[:, 1 + x, :, :],
                          A["L0_ffn_experts_w2"][x].rearrange("(k p) d -> p k d", p=128))
            d_f.start(sp, f_g[:, :], A["L0_ffn_gate_w"])
            wf = d_f.mark()
            xn = ar[:, 0:2048].rearrange("p (b d) -> p b d", b=NB)
            ln = layernorm(xn, [])
            zero = pool.do(lambda e: e.memset(g3[:, :], 0.0))
            rk = None
            for x in range(8):
                rk = pool.do(lambda e, x=x: e.memset(rank[:, :, x], 8.0 - x))
            for b in range(NB):
                t = mm(bank(2)[:, 8 * b:8 * b + 8], XN[:, 128 * b:128 * b + 128], f_g[:, :], True, True, wf, ln[b // 4],
                       sig=True)
            m = dve.do(lambda e: e.tensor_copy(lg[:, :, :].rearrange("p b x -> p (b x)"), bank(2)[:, 0:128]), t)

            def bc(v):
                return v.unsqueeze(2).to_broadcast([128, NB, 8])

            def first_max(src, mv_, onehot, m):
                m = dve.do(lambda e: e.tensor_reduce(mv_, src, AX.X, ALU.max), m)
                m = dve.do(lambda e: e.tensor_tensor(tmp[:, :, :], src, bc(mv_), ALU.is_equal), m)
                m = dve.do(lambda e: e.tensor_tensor(tmp[:, :, :], tmp[:, :, :], rank[:, :, :], ALU.mult), m, rk)
                m = dve.do(lambda e: e.tensor_reduce(mx[:, 2, :], tmp[:, :, :], AX.X, ALU.max), m)
                return dve.do(lambda e: e.tensor_tensor(onehot, tmp[:, :, :], bc(mx[:, 2, :]), ALU.is_equal), m)

            m = first_max(lg[:, :, :], mx[:, 0, :], oh[:, :, :], m)
            m = dve.do(lambda e: e.scalar_tensor_tensor(out=lg[:, :, :], in0=oh[:, :, :], scalar=-3.0e38,
                                                        in1=lg[:, :, :], op0=ALU.mult, op1=ALU.add), m)
            m = first_max(lg[:, :, :], mx[:, 1, :], G[:, :, :], m)
            m = dve.do(lambda e: e.tensor_tensor(mx[:, 2, :], mx[:, 1, :], mx[:, 0, :], ALU.subtract), m)
            m = act.do(lambda e: e.activation(mx[:, 2, :], mx[:, 2, :], ACT.Exp), m)
            m = dve.do(lambda e: e.tensor_scalar(mx[:, 3, :], mx[:, 2, :], 1.0, None, ALU.add), m)
            m = dve.do(lambda e: e.reciprocal(mx[:, 3, :], mx[:, 3, :]), m)
            m = dve.do(lambda e: e.tensor_tensor(mx[:, 2, :], mx[:, 2, :], mx[:, 3, :], ALU.mult), m)
            m = dve.do(lambda e: e.tensor_tensor(oh[:, :, :], oh[:, :, :], bc(mx[:, 3, :]), ALU.mult), m)
            m = dve.do(lambda e: e.tensor_tensor(G[:, :, :], G[:, :, :], bc(mx[:, 2, :]), ALU.mult), m)
            m = dve.do(lambda e: e.tensor_tensor(G[:, :, :], G[:, :, :], oh[:, :, :], ALU.add), m)
            mg = spread(G, ar[:, 2048:4096], g3, ar[:, 4096:6144], ar[:, 6144:8192], zero, m)
            meet()
            h = ar[:, 0:1536].rearrange("p (a b) -> p a b", a=3)
            hg = ar[:, 1536:3072].rearrange("p (a b) -> p a b", a=3)
            hid = dict(rows=[None] + list(range(8)), f=ACT.Silu, o=ar[:, 3072:3584], done=lambda q, m: None)
            moe(lambda e_, j: f_w1[:, e_, 128 * j:128 * j + 128], lambda e_, j: f_w2[:, e_, j, :], g3, [mg], 9,
                h, hg, hid, lambda e_, j: 0.0, None, wf)
            meet()

        def stage3(ph):
            def sa(name, shape, dt=F32):
                return sb(name, shape, dt, ph)

            d_w = loads("d_w")
            W = {}
            for nm in ("Wq", "Wk", "Wv", "out"):
                W[nm] = sa("w_" + nm + "1", [128, 128])
                d_w.start(sp, W[nm][:, :], A[f"L1_attn_{nm}_w"])
            for nm in ("convq", "convk"):
                W[nm] = sa("w_" + nm, [128, 3, 128])
                d_w.start(sp, W[nm][:, :, :], A[f"L1_attn_{nm}_w"])
            for nm in ("qproj", "kproj"):
                W[nm] = sa("w_" + nm, [128, 2, 128])
                d_w.start(sp, W[nm][:, :, :], A[f"L1_attn_{nm}_w"].rearrange("(g p) n -> p g n", p=128))
            cols = sa("cols", [128, 8])
            d_w.start(sp, cols[:, :], A["cols"])
            t1w = sa("t1w", [128, 2, 2, 4])
            d_w.start(sp, t1w[:, :, :, :], A["t1w"])
            t2w = sa("t2w", [128, 2, 128])
            d2w = sa("d2w", [128, 2, 16])
            d_w.start(sp, t2w[:, :, :], A["L1_attn_tau2_w"].rearrange("(p g) n -> p g n", g=2))
            d_w.start(sp, d2w[:, :, :], A["L1_attn_del2_w"].rearrange("(p g) n -> p g n", g=2))
            bb = sa("bb", [128, 2, 128])
            d_w.start(sp, bb[:, 0, :], A["L1_attn_Wv_b"].partition_broadcast(128))
            d_w.start(sp, bb[:, 1, :], A["L1_attn_out_b"].partition_broadcast(128))
            ww = d_w.mark()

            tauR = sa("tauR", [128, T])
            va = sa("va", [128, NB, NH, 32])
            QS = sa("QS", [128, 8, T], BF16)
            KS = sa("KS", [128, 8, T], BF16)
            aa = sa("aa", [128, 12288])
            mxh = sa("mxh", [128, NB, NH])

            zq = dve.do(lambda e: e.memset(va[:, :, :, :], 0.0))
            zq = dve.do(lambda e: e.memset(va[:, :, :, 8:9], 1.0), zq)
            z1 = pool.do(lambda e: e.memset(QS[:, :, :], 1.0))
            z2 = pool.do(lambda e: e.memset(KS[:, :, :], 1.0))
            ln = layernorm(aa[:, 0:2048].rearrange("p (b d) -> p b d", b=NB), [])
            delT = aa[0:16, 10240:12288]
            free = [None] * 8
            prev = []
            mm_tau = None
            for i in range(2):
                gl = []
                for g in range(2):
                    cvt = aa[:, 2048 + 2048 * g:4096 + 2048 * g]
                    m = dve.do(lambda e, i=i, g=g, c=cvt: e.tensor_scalar(
                        c, xnT[:, 0:T], t1w[:, i, g, 0:1], t1w[:, i, g, 3:4], ALU.mult, ALU.add), ww, ln[3], *prev)
                    for j in (1, 2):
                        m = dve.do(lambda e, i=i, g=g, j=j, c=cvt: e.scalar_tensor_tensor(
                            out=c, in0=xnT[:, j:j + T], scalar=t1w[:, i, g, j:j + 1], in1=c,
                            op0=ALU.mult, op1=ALU.add), m)
                    gl.append(act.do(lambda e, c=cvt: e.activation(c, c, ACT.Gelu), m))
                prev = []
                for q in range(4):
                    s = slice(512 * q, 512 * q + 512)
                    k = 2 + q
                    w2, o, bcol, M = ((t2w, tauR, cols[:, 6:7], 128), (d2w, delT, cols[0:16, 7:8], 16))[i]
                    for g in range(2):
                        t = mm(bank(k)[0:M, :], w2[:, g, :], aa[:, 2048 + 2048 * g + 512 * q:2560 + 2048 * g + 512 * q],
                               g == 0, g == 1, gl[g], free[k], ww, sig=True)
                    prev.append(t)
                    free[k] = act.do(lambda e, o=o, s=s, k=k, M=M, bcol=bcol: e.activation(
                        o[:, s], bank(k)[0:M, :], ACT.Sigmoid, bias=bcol), t)
                    last = free[k]
            mtau = last
            sc = scratch("sc", [7, 128, T], BF16)
            d_s = loads("d_s")
            rr1, rr2 = aa[:, 6144:8192], aa[:, 8192:10240]
            parts = aa[:, 0:3072].bitcast(BF16).rearrange("p (k t) -> p k t", k=3)
            m = split3(None, delT, [parts[0:16, k, :] for k in range(3)], rr1[0:16, :], rr2[0:16, :], last, *prev)
            d_r = loads("d_r")
            for hh in range(2):
                for k in range(3):
                    src = parts[0:16, k, :]
                    d_s.start(sp, sc[6, 16 * k:16 * k + 16, :], src, m) if hh == 0 else None
            mds = d_s.mark()
            for hh in range(2):
                for k in range(3):
                    srcd = sc[6, 16 * k:16 * k + 16, :].rearrange("(a b) t -> b a t", b=2)[hh:hh + 1, :, :]
                    d_r.start(sp, KS[64 * hh + 48 + k:64 * hh + 49 + k, :, :], srcd, mds, z1, z2)
            grp = ([0, 1, 0, 1, 2, 0], [0, 0, 1, 1, 0, 2])
            pd = aa[:, 0:T + 2]
            mprev = [mds, m]
            for i, (wn, cn, pn) in enumerate((("Wq", "convq", "qproj"), ("Wk", "convk", "kproj"))):
                pd = aa[:, 3072:3072 + T + 2]
                c3 = aa[:, 5200:5200 + T]
                qv = aa[:, 7300:7300 + T]
                sr = aa[:, 9400:9400 + T]
                z = [dve.do(lambda e: e.memset(pd[:, 0:1], 0.0), *mprev),
                     dve.do(lambda e: e.memset(pd[:, T + 1:T + 2], 0.0), *mprev)]
                ev_ = []
                for q in range(4):
                    k = 2 + q
                    t = mm(bank(k), W[wn][:, :], XN[:, 512 * q:512 * q + 512], True, True, free[k], sig=True)
                    free[k] = act.do(lambda e, k=k, q=q, i=i: e.activation(
                        pd[:, 1 + 512 * q:513 + 512 * q], bank(k), ACT.Identity, bias=cols[:, i:i + 1]), t, z)
                    ev_.append(free[k])
                ev2 = []
                for q in range(4):
                    k = 2 + q
                    for j in range(3):
                        t = mm(bank(k), W[cn][:, j, :], pd[:, 512 * q + j:512 * q + j + 512], j == 0, j == 2,
                               free[k], ev_, sig=(j == 2))
                    free[k] = act.do(lambda e, k=k, q=q, i=i: e.activation(
                        c3[:, 512 * q:512 * q + 512], bank(k), ACT.Identity, bias=cols[:, 2 + i:3 + i]), t)
                    ev2.append(free[k])
                ev3 = []
                for q in range(4):
                    k = 2 + q
                    mm(bank(k), W[pn][:, 0, :], pd[:, 1 + 512 * q:513 + 512 * q], True, False, free[k], ev2)
                    t = mm(bank(k), W[pn][:, 1, :], c3[:, 512 * q:512 * q + 512], False, True, sig=True)
                    free[k] = act.do(lambda e, k=k, q=q, i=i: e.activation(
                        qv[:, 512 * q:512 * q + 512], bank(k), ACT.Identity, bias=cols[:, 4 + i:5 + i]), t)
                    ev3.append(free[k])
                m = ev3[-1]
                if i == 0:
                    m = dve.do(lambda e: e.scalar_tensor_tensor(out=qv, in0=qv, scalar=float(8.0 ** -0.5),
                                                                in1=tauR[:, :], op0=ALU.mult, op1=ALU.mult), m, mtau)
                mprev2 = split3(None, qv, [parts[:, k, :] for k in range(3)], c3, sr, m, *mprev, t)
                for k in range(3):
                    d_s.start(sp, sc[3 * i + k, :, :], parts[:, k, :], mprev2)
                mds = d_s.mark()
                mprev = [mds, mprev2]
                dst = (QS, KS)[i]
                for hh in range(2):
                    for gi, pk in enumerate(grp[i]):
                        srcd = sc[3 * i + pk].rearrange("(a b r) t -> b r a t", b=2, r=8)[hh]
                        d_r.start(sp, dst[64 * hh + 8 * gi:64 * hh + 8 * gi + 8, :, :], srcd, mds, z1, z2)
            mqk = d_r.mark()
            for q in range(4):
                k = 2 + q
                for b in range(4):
                    tb = 4 * q + b
                    t = mm(bank(k)[:, 128 * b:128 * b + 128], XN[:, 128 * tb:128 * tb + 128], W["Wv"][:, :],
                           True, True, free[k], sig=True)
                for b in range(4):
                    tb = 4 * q + b
                    m = dve.do(lambda e, k=k, b=b, tb=tb: e.tensor_tensor(
                        va[:, tb, :, 0:8], bank(k)[:, 128 * b:128 * b + 128].rearrange("p (h r) -> p h r", h=16),
                        bb[:, 0, :].rearrange("p (h r) -> p h r", h=16), ALU.add), t, zq)
                free[k] = m
            mva = m
            meet()
            Pt = [aa[:, 1024 * i:1024 * i + 1024] for i in range(3)]
            Oe = [aa[:, 3072 + 512 * i:3584 + 512 * i] for i in range(2)]
            nm = aa[0:16, 4096:4608]
            n1, n2 = aa[0:16, 4608:5120], aa[0:16, 5120:5632]
            n3 = [aa[0:16, 5632 + 256 * k:5888 + 256 * k].bitcast(BF16) for k in range(3)]
            rs = aa[:, 6400:6464]
            at = aa[:, 6656:8704].rearrange("p (b d) -> p b d", b=NB)
            att = aa[:, 8704:9216]
            fS = [None] * 2
            fP = [None] * 3
            fO = [None] * 1
            fOe = [None] * 2
            fM = [None] * 2
            fMr = None
            d_n = loads("d_n")
            i1 = 0

            def maxima(qb):
                nonlocal i1
                m = None
                for h in range(NH):
                    hh, pr = h % 2, h // 2
                    p0 = 64 * hh
                    for c in range(4):
                        if c % 2 == 0:
                            bk = 4 + 0
                        t = mm(bank(4 + c % 2), QS[p0:p0 + 51, pr, 128 * qb:128 * qb + 128],
                               KS[p0:p0 + 51, pr, 512 * c:512 * c + 512], True, True, fM[c % 2], mqk, mmt[0], sig=True)
                        fM[c % 2] = dve.do(lambda e, h=h, qb=qb, c=c: e.tensor_reduce(
                            mx4[:, h, c:c + 1], bank(4 + c % 2), AX.X, ALU.max), t)
                return dve.do(lambda e, qb=qb: e.tensor_reduce(mxh[:, qb, :], mx4[:, :, :], AX.X, ALU.max,
                                                               negate=True), fM[0], fM[1])

            mx4 = sa("mx4", [128, NH, 4])
            mmt = [None]
            for qc in range(4):
                for b in range(4):
                    m = maxima(4 * qc + b)
                    t = pe.do(lambda e, b=b, qb=4 * qc + b: e.transpose(bank(7)[0:16, 128 * b:128 * b + 128],
                                                                        mxh[:, qb, :], ident[:, :]), m, fMr)
                fMr = act.do(lambda e: e.activation(nm, bank(7)[0:16, :], ACT.Copy), t, d_n.mark() if qc else None)
                m = split3(None, nm, n3, n1, n2, fMr)
                if qc == 0:
                    pass
                qs = slice(512 * qc, 512 * qc + 512)
                for k in range(3):
                    d_n.start(sp, sc[6, 48 + 16 * k:64 + 16 * k, qs], n3[k], m)
                mn = d_n.mark()
                for hh in range(2):
                    for k in range(3):
                        srcd = sc[6, 48 + 16 * k:64 + 16 * k, qs].rearrange("(a b) t -> b a t", b=2)[hh:hh + 1, :, :]
                        d_n.start(sp, QS[64 * hh + 51 + k:64 * hh + 52 + k, :, qs], srcd, mn)
                mn = d_n.mark()
                for hg in range(4):
                    pend = []

                    def pv(item):
                        kb, pp, pt, m = item
                        for hh in range(2):
                            j = 2 * pp + hh
                            t = pe.do(lambda e, j=j, kb=kb, pt=pt, hh=hh, hg=hg: e.matmul(
                                bank(6)[32 * j:32 * j + 32, :], va[:, kb, 4 * hg + j, :],
                                pt[:, 512 * hh:512 * hh + 512], start=(kb == 0), stop=(kb == NB - 1)), m, fO[0], mva)
                        return t

                    it = 0
                    for kb in range(NB):
                        for pp in range(2):
                            pr = 2 * hg + pp
                            for hh in range(2):
                                p0 = 64 * hh
                                t = mm(bank(2 * (it % 2) + hh), KS[p0:p0 + 54, pr, 128 * kb:128 * kb + 128],
                                       QS[p0:p0 + 54, pr, qs], True, True, fS[it % 2], mn, sig=True)
                            pt = Pt[it % 3]
                            m = act.do(lambda e, pt=pt, k=it % 2: e.activation(pt, bank(2 * k, 2), ACT.Exp), t,
                                       fP[it % 3])
                            fS[it % 2] = m
                            pend.append((kb, pp, pt, m, it))
                            it += 1
                            if len(pend) > 1:
                                x = pend.pop(0)
                                fP[x[4] % 3] = pv(x[:4])
                    while pend:
                        x = pend.pop(0)
                        tl = pv(x[:4])
                        fP[x[4] % 3] = tl
                    oe = Oe[hg % 2]
                    m = dve.do(lambda e, oe=oe: e.tensor_copy(oe, bank(6)), tl, fOe[hg % 2])
                    fO[0] = m
                    for b in range(4):
                        tt = pe.do(lambda e, b=b, oe=oe: e.transpose(bank(7)[:, 128 * b:128 * b + 128],
                                                                     oe[:, 128 * b:128 * b + 128], ident[:, :]),
                                   m, fMr)
                    fOe[hg % 2] = tt
                    v7 = bank(7).rearrange("p (b h c) -> p b h c", b=4, h=4)
                    rv = rs[:, 0:16].rearrange("p (b h o) -> p b h o", b=4, h=4)
                    m = dve.do(lambda e, v7=v7, rv=rv: e.reciprocal(rv, v7[:, :, :, 8:9]), tt)
                    for b in range(4):
                        m2 = dve.do(lambda e, v7=v7, rv=rv, b=b, hg=hg, qc=qc: e.tensor_tensor(
                            at[:, 4 * qc + b, 32 * hg:32 * hg + 32].rearrange("p (h r) -> p h r", h=4),
                            v7[:, b, :, 0:8], rv[:, b, :, :].to_broadcast([128, 4, 8]), ALU.mult), m)
                    fMr = m2
                for b in range(4):
                    tt = pe.do(lambda e, b=b, qc=qc: e.transpose(bank(7)[:, 128 * b:128 * b + 128],
                                                                 at[:, 4 * qc + b, :], ident[:, :]), fMr)
                m = act.do(lambda e: e.activation(att, bank(7), ACT.Copy), tt, mmt[0])
                for b in range(4):
                    t = mm(bank(7)[:, 128 * b:128 * b + 128], att[:, 128 * b:128 * b + 128], W["out"][:, :],
                           True, True, m, sig=True)
                xs = x_tok[:, 4 * qc:4 * qc + 4, :]
                b7 = bank(7).rearrange("p (b d) -> p b d", b=4)
                m = dve.do(lambda e, xs=xs, b7=b7: e.tensor_tensor(xs, xs, b7, ALU.add), t)
                fMr = m
                for b in range(4):
                    m = dve.do(lambda e, b=b, qc=qc: e.tensor_tensor(
                        x_tok[:, 4 * qc + b, :], x_tok[:, 4 * qc + b, :], bb[:, 1, :], ALU.add), m)
                mmt[0] = t
            meet()

        def stage4(ph):
            def sa(name, shape, dt=F32):
                return sb(name, shape, dt, ph)

            d_g = loads("d_g")
            h_w1 = sa("h_w1", [128, 8, 512])
            h_w2 = sa("h_w2", [128, 8, 4, 128])
            h_b1 = sa("h_b1", [128, 8, 4])
            h_b2 = sa("h_b2", [8, 128])
            d_g.start(sp, h_w1[:, :, :], A["L1_ffn_W1"].rearrange("e d h -> d e h"))
            for x in range(8):
                d_g.start(sp, h_w2[:, x, :, :], A["L1_ffn_W2"][x].rearrange("(k p) d -> p k d", p=128))
            d_g.start(sp, h_b1[:, :, :], A["L1_ffn_b1"])
            d_g.start(sp, h_b2[:, :], A["L1_ffn_b2"])
            wg = d_g.mark()
            ar = sa("ar2", [128, 10240])
            g3 = sa("g32", [96, T], BF16)
            kk = sa("kk", [128, NB, 16])
            c16 = sa("c16", [128, NB, 16])
            sv = sa("sv", [128, 4, NB])
            eA = sa("eA", [128, 2, NB, 8])
            G = sa("Gh", [128, NB, 8])
            G2 = sa("Gh2", [128, NB, 8])
            xn = ar[:, 0:2048].rearrange("p (b d) -> p b d", b=NB)
            cm = None
            for x in range(16):
                cm = pool.do(lambda e, x=x: e.memset(kk[:, :, x], float(x + 1)))
            for x in range(8):
                cm = pool.do(lambda e, x=x: e.memset(eA[:, 0, :, x], float(x)))
                cm = pool.do(lambda e, x=x: e.memset(eA[:, 1, :, x], float((x + 7) % 8)))
            zero = pool.do(lambda e: e.memset(g3[:, :], 0.0))
            ln = layernorm(xn, [])
            s_, tr, a_, b_ = (sv[:, i, :] for i in range(4))
            m = dve.do(lambda e: e.tensor_tensor(s_, xn[:, :, 0], xn[:, :, 1], ALU.add), ln[3])

            def count(dst, src, op, n, lane_m):
                m = dve.do(lambda e: e.tensor_tensor(c16[:, :, 0:n], src.unsqueeze(2).to_broadcast([128, NB, n]),
                                                     kk[:, :, 0:n], op), lane_m, cm)
                return dve.do(lambda e: e.tensor_reduce(dst, c16[:, :, 0:n], AX.X, ALU.add), m)

            m = count(a_, s_, ALU.is_ge, 16, m)
            m = dve.do(lambda e: e.tensor_scalar(s_, s_, -1.0, None, ALU.mult), m)
            m = count(b_, s_, ALU.is_ge, 16, m)
            m = dve.do(lambda e: e.tensor_tensor(tr, a_, b_, ALU.subtract), m)
            m = dve.do(lambda e: e.tensor_scalar(a_, tr, 16.0, 0.125, ALU.add, ALU.mult), m)
            m = count(b_, a_, ALU.is_ge, 4, m)
            m = dve.do(lambda e: e.scalar_tensor_tensor(out=tr, in0=b_, scalar=-8.0, in1=tr, op0=ALU.mult,
                                                        op1=ALU.add), m)
            m = dve.do(lambda e: e.tensor_scalar(tr, tr, 16.0, None, ALU.add), m)
            hb_ = tr.unsqueeze(2).to_broadcast([128, NB, 8])
            m = dve.do(lambda e: e.tensor_tensor(G[:, :, :], eA[:, 0, :, :], hb_, ALU.is_equal), m)
            m = dve.do(lambda e: e.tensor_tensor(G2[:, :, :], eA[:, 1, :, :], hb_, ALU.is_equal), m)
            m = dve.do(lambda e: e.tensor_tensor(G[:, :, :], G[:, :, :], G2[:, :, :], ALU.add), m)
            m = dve.do(lambda e: e.tensor_scalar(G[:, :, :], G[:, :, :], 0.5, None, ALU.mult), m)
            gT = ar[:, 8192:10240]
            mg = spread(G, gT, g3, ar[:, 4096:6144], ar[:, 6144:8192], zero, m)
            meet()
            h = ar[:, 0:1536].rearrange("p (a b) -> p a b", a=3)
            hg = ar[:, 1536:3072].rearrange("p (a b) -> p a b", a=3)
            d_o = loads("d_o")
            ov = out.rearrange("o (b p) d -> p (o b) d", p=128)

            def done(q, m):
                d_o.start(sp, ov[:, 4 * q:4 * q + 4, :], x_tok[:, 4 * q:4 * q + 4, :], m)

            hid = dict(rows=list(range(8)), f=ACT.Relu, o=ar[:, 3072:3584], done=done)
            moe(lambda e_, j: h_w1[:, e_, 128 * j:128 * j + 128], lambda e_, j: h_w2[:, e_, j, :], g3, [mg], 8,
                h, hg, hid, lambda e_, j: h_b1[:, e_, j:j + 1],
                lambda o, s: mm(o, h_b2[:, :], gT[0:8, s], False, True, sig=True), wg)
            sp.wait(d_o.mark())

        for n, stage in enumerate((stage1, stage2, stage3, stage4)):
            with ExitStack() as ph:
                stage(ph)
            if DEBUG == n + 1:
                finish(ctx, nc, lanes, x_tok, out, loads, meet)
                return
        play(ctx, nc, lanes)


def play(ctx, nc, lanes):
    pe, act, dve, pool, sp = lanes
    block = ctx.enter_context(nc.Block())

    @block.tensor
    def _(e):
        pe.play(e)

    @block.scalar
    def _(e):
        act.play(e)

    @block.vector
    def _(e):
        dve.play(e)

    @block.gpsimd
    def _(e):
        pool.play(e)

    @block.sync
    def _(e):
        sp.play(e)


def finish(ctx, nc, lanes, x_tok, out, loads, meet):
    d_o = loads("d_o")
    meet()
    d_o.start(lanes[4], out.rearrange("o (b p) d -> p (o b) d", p=128), x_tok[:, :, :])
    lanes[4].wait(d_o.mark())
    play(ctx, nc, lanes)


DEBUG = 0


def kernel(**inputs):
    import numpy as _np
    import concourse.bacc as _bacc
    from concourse import mybir as _mybir
    from concourse.bass_utils import run_bass_kernel_spmd as _run

    a = {k: _np.asarray(v) for k, v in inputs.items()}
    lay = dict(a)
    for n in ("L0_attn_conv_b", "L0_attn_dt_b", "L0_attn_D_param"):
        lay[n] = a[n].reshape(2, 128).T
    lay["L0_ffn_shared_w1"] = a["L0_ffn_shared_w1"].T
    lay["L0_ffn_shared_w2"] = a["L0_ffn_shared_w2"].T
    lay["L0_ffn_experts_w1"] = a["L0_ffn_experts_w1"].transpose(0, 2, 1)
    lay["L0_ffn_experts_w2"] = a["L0_ffn_experts_w2"].transpose(0, 2, 1)
    lay["L0_ffn_gate_w"] = a["L0_ffn_gate_w"].T
    for n in ("Wq_w", "Wk_w", "Wv_w", "out_w", "qproj_w", "kproj_w"):
        lay["L1_attn_" + n] = a["L1_attn_" + n].T
    for n in ("convq_w", "convk_w"):
        lay["L1_attn_" + n] = a["L1_attn_" + n].transpose(1, 2, 0)
    rep = _np.repeat(a["L1_attn_tau2_b"], 8)
    lay["cols"] = _np.stack([lay.pop("L1_attn_" + n) for n in ("Wq_b", "Wk_b", "convq_b", "convk_b", "qproj_b",
                                                              "kproj_b")]
                            + [rep, _np.pad(lay.pop("L1_attn_del2_b"), (0, 112))], axis=1)
    lay.pop("L1_attn_tau2_b")
    lay["t1w"] = _np.stack([_np.concatenate([lay.pop(f"L1_attn_{n}_w").reshape(128, 2, 3),
                                             lay.pop(f"L1_attn_{n}_b").reshape(128, 2, 1)], axis=2)
                            for n in ("tau1", "del1")], axis=1)
    lay["L1_attn_tau2_w"] = _np.repeat(a["L1_attn_tau2_w"][:, :, 0], 8, axis=0).T
    lay["L1_attn_del2_w"] = a["L1_attn_del2_w"][:, :, 0].T
    lay["L1_ffn_b1"] = a["L1_ffn_b1"].reshape(8, 4, 128).transpose(2, 0, 1)
    nc = _bacc.Bacc("TRN2", target_bir_lowering=False, num_devices=1)
    arrays, aps = {}, {}
    for n, v in lay.items():
        v = _np.ascontiguousarray(v)
        arrays[f"in_{n}"] = v
        aps[n] = nc.dram_tensor(f"in_{n}", v.shape, _mybir.dt.from_np(v.dtype), kind="ExternalInput").ap()
    o = nc.dram_tensor("out_0", (1, 2048, 128), _mybir.dt.float32, kind="ExternalOutput").ap()
    build(nc, aps, o)
    r = _run(nc, [arrays], core_ids=[0])
    return r.results[0]["out_0"]
```

```python
from contextlib import ExitStack

import concourse.bass as bass
import numpy as np
from concourse import mybir

ALU = mybir.AluOpType
ACT = mybir.ActivationFunctionType
AX = mybir.AxisListType
F32 = mybir.dt.float32
BF16 = mybir.dt.bfloat16

T = 2048
NB = T // 128
NE = 8
NH = 16
TQ = 1024
E20 = float(np.float32(np.exp(20.0)))
LOG1P = [0.9999999992732804, -0.49999981737027194, 0.3333256943206084, -0.24987395019953507,
         0.1989154870228832, -0.16108664975266748, 0.12425163151193669, -0.08253601410389311,
         0.04155808633524785, -0.013445002542276745, 0.002037716592261226]


class Lane:

    def __init__(self, name, sem):
        self.name, self.sem, self.count, self.seen, self.items = name, sem, 0, {}, []

    def wait(self, *marks):
        for m in marks:
            if m is None:
                continue
            if isinstance(m, list):
                self.wait(*m)
                continue
            sem, value = m
            if self.seen.get(sem.name, 0) < value:
                self.seen[sem.name] = value
                self.items.append(lambda e, s=sem, v=value: e.wait_ge(s, v))

    def do(self, fn, *marks):
        self.wait(*marks)
        self.count += 1
        self.items.append(lambda e, s=self.sem: fn(e).then_inc(s, 1))
        return (self.sem, self.count)

    def quiet(self, fn, *marks):
        self.wait(*marks)
        self.items.append(lambda e: fn(e))

    def play(self, e):
        for item in self.items:
            item(e)


class Loads:

    def __init__(self, sem):
        self.sem, self.count = sem, 0

    def start(self, lane, out, in_, *marks):
        lane.wait(*marks)
        self.count += 16
        lane.items.append(lambda e: e.dma_start(out, in_).then_inc(self.sem, 16))

    def mark(self):
        return (self.sem, self.count)


def build(nc, A, out):
    with ExitStack() as ctx:
        def sem(name):
            return ctx.enter_context(nc.semaphore(name))

        pe, act, dve, pool, sp = (Lane(n, sem("s_" + n)) for n in ("pe", "act", "dve", "pool", "sp"))
        lanes = (pe, act, dve, pool, sp)
        used = [0]

        def sb(name, shape, dt=F32, stack=ctx):
            return stack.enter_context(nc.sbuf_tensor(name, shape, dt))

        def loads(name):
            return Loads(sem(name))

        def scratch(name, shape, dt):
            return nc.dram_tensor(name, shape, dt, kind="Internal").ap()

        PS = ctx.enter_context(nc.psum_tensor("PS", [128, 8, 512], F32))

        def bank(i, n=1):
            return PS[:, i, :] if n == 1 else PS[:, i:i + n, :].rearrange("p a b -> p (a b)")

        def meet():
            marks = [(x.sem, x.count) for x in lanes if x.count]
            for x in lanes:
                x.wait(*marks)

        x_tok = sb("x_tok", [128, NB, 128])
        xnT = sb("xnT", [128, T + 2])
        XN = xnT[:, 1:T + 1]
        ident = sb("ident", [128, 128])
        identb = sb("identb", [128, 128], BF16)
        sel = sb("sel", [96, 32, 128], BF16)
        cst = sb("cst", [128, 4])
        st6 = sb("st6", [128, NB, 6])
        mv = sb("mv", [128, NB, 2])
        rstd = sb("rstd", [128, NB])
        mhalf = sb("mhalf", [128, NB])

        d_x = loads("d_x")
        d_a = loads("d_a")
        d_f = loads("d_f")
        xv = A["L0_attn_x"].rearrange("o (b p) d -> p (o b) d", p=128)
        d_x.start(sp, x_tok[:, :, :], xv)

        c0 = pool.do(lambda e: e.memset(ident[:, :], 0.0))
        c1 = pool.do(lambda e: e.affine_select(out=ident[:, :], in_=ident[:, :], compare_op=ALU.not_equal, fill=1.0,
                                               base=0, pattern=[[-1, 128]], channel_multiplier=1), c0)
        s0 = pool.do(lambda e: e.memset(sel[:, :, :], 0.0))
        for k in range(3):
            s0 = pool.do(lambda e, k=k: e.affine_select(
                out=sel[:, :, :], in_=sel[:, :, :], compare_op=ALU.not_equal, fill=1.0,
                base=-32 * k, pattern=[[-1, 32], [0, 128]], channel_multiplier=1), s0)
        c_sel = s0
        c2 = pool.do(lambda e: e.memset(mhalf[:, :], -0.5))
        c3 = dve.do(lambda e: e.memset(xnT[:, 0:1], 0.0))
        c4 = dve.do(lambda e: e.memset(xnT[:, T + 1:T + 2], 0.0))
        c_const = [c1, c_sel, c2, c3, c4]

        def split3(lane_src, src, outs, r1, r2, *marks):
            m = dve.do(lambda e: e.tensor_copy(outs[0], src), *marks)
            m1 = dve.do(lambda e: e.tensor_tensor(r1, src, outs[0], ALU.subtract), m)
            m = dve.do(lambda e: e.tensor_copy(outs[1], r1), m1)
            m2 = dve.do(lambda e: e.tensor_tensor(r2, r1, outs[1], ALU.subtract), m)
            return dve.do(lambda e: e.tensor_copy(outs[2], r2), m2)

        def layernorm(xn, after, bank0=0, keep=None):
            m = None
            for b in range(NB):
                m = dve.do(lambda e, b=b: e.bn_stats(st6[:, b, :], x_tok[:, b, :]), *after)
            ms = [dve.do(lambda e, b=b: e.bn_aggr(mv[:, b, :], st6[:, b, :]), m) for b in range(NB)]
            m = dve.do(lambda e: e.tensor_scalar(rstd[:, :], mv[:, :, 1], 1e-5, None, ALU.add), ms[-1])
            m = pool.do(lambda e: e.tensor_tensor(rstd[:, :], rstd[:, :], mhalf[:, :], ALU.pow), m, c2)
            done = []
            free = [None, None]
            for q in range(4):
                for b in range(4 * q, 4 * q + 4):
                    n = dve.do(lambda e, b=b: e.tensor_scalar(xn[:, b, :], x_tok[:, b, :], mv[:, b, 0:1],
                                                              rstd[:, b:b + 1], ALU.subtract, ALU.mult), m)
                for b in range(4 * q, 4 * q + 4):
                    t = pe.do(lambda e, b=b, q=q: e.transpose(bank(bank0 + q % 2)[:, (b % 4) * 128:(b % 4 + 1) * 128],
                                                              xn[:, b, :], ident[:, :]), n, free[q % 2], c1)
                free[q % 2] = act.do(lambda e, q=q: e.activation(XN[:, 512 * q:512 * q + 512], bank(bank0 + q % 2),
                                                                 ACT.Copy), t)
                done.append(free[q % 2])
            return done

        def mm(o, l, r, start, stop, *marks, sig=False):
            f = pe.do if sig else pe.quiet
            return f(lambda e: e.matmul(o, l, r, start=start, stop=stop), *marks)

        def stage1(ph):
            def sa(name, shape, dt=F32):
                return sb(name, shape, dt, ph)

            w_in = sa("w_in", [128, 512])
            w_cv = sa("w_cv", [128, 2, 4])
            w_cb = sa("w_cb", [128, 2])
            w_xp = sa("w_xp", [128, 2, 33])
            w_dt = sa("w_dt", [33, 256])
            w_db = sa("w_db", [128, 2])
            w_al = sa("w_al", [128, 2, 16])
            w_D = sa("w_D", [128, 2])
            w_out = sa("w_out", [128, 2, 128])
            Am = sa("Am", [128, 32])
            u = sa("u", [128, 2, T])
            zs = sa("zs", [128, 2, T])
            dl = sa("dl", [128, 2, T])
            du = sa("du", [128, 2, T])
            ssm3 = sa("ssm3", [96, T], BF16)
            hl = sa("hl", [128, 32])
            arena = sa("arena", [128, 20480])
            d_a.start(sp, w_in[:, :], A["L0_attn_in_proj_w"])
            d_a.start(sp, w_cv[:, :, :], A["L0_attn_conv_w"].rearrange("(g p) o k -> p g (o k)", p=128))
            d_a.start(sp, w_cb[:, :], A["L0_attn_conv_b"])
            d_a.start(sp, w_xp[:, :, :], A["L0_attn_x_proj_w"].rearrange("(g p) n -> p g n", p=128))
            d_a.start(sp, w_dt[32:33, :], A["L0_attn_dt_w"])
            d_a.start(sp, w_db[:, :], A["L0_attn_dt_b"])
            d_a.start(sp, w_al[:, :, :], A["L0_attn_A_log"].rearrange("(g p) n -> p g n", p=128))
            d_a.start(sp, w_D[:, :], A["L0_attn_D_param"])
            d_a.start(sp, w_out[:, :, :], A["L0_attn_out_proj_w"].rearrange("(g p) n -> p g n", p=128))
            wa = d_a.mark()

            xn = arena[:, 0:2048].rearrange("p (b d) -> p b d", b=NB)
            ln = layernorm(xn, [d_x.mark()])
            xin = arena[:, 2048:2048 + 2 * (T + 3)].rearrange("p (g t) -> p g t", g=2)
            cv = arena[:, 8192:8192 + 2 * T].rearrange("p (g t) -> p g t", g=2)
            z0 = dve.do(lambda e: e.memset(xin[:, :, 0:3], 0.0))
            mA = act.do(lambda e: e.activation(Am[:, :], w_al[:, :, :].rearrange("p g n -> p (g n)"), ACT.Exp), wa)
            mA = act.do(lambda e: e.mul(Am[:, :], Am[:, :], -1.0), mA)
            free = [None] * 8
            ev = {}
            for i, (m, q) in enumerate([(m, q) for m in range(4) for q in range(4)]):
                k = 2 + i % 4
                t = mm(bank(k), w_in[:, 128 * m:128 * m + 128], XN[:, 512 * q:512 * q + 512], True, True,
                       wa, ln[q], free[k], sig=True)
                if m < 2:
                    o = xin[:, m, 3 + 512 * q:3 + 512 * q + 512]
                    free[k] = act.do(lambda e, o=o, k=k: e.activation(o, bank(k), ACT.Copy), t)
                else:
                    o = zs[:, m - 2, 512 * q:512 * q + 512]
                    free[k] = act.do(lambda e, o=o, k=k: e.activation(o, bank(k), ACT.Silu), t)
                ev[m, q] = free[k]
            mu = []
            for g in range(2):
                m = dve.do(lambda e, g=g: e.tensor_scalar(cv[:, g, :], xin[:, g, 0:T], w_cv[:, g, 0:1],
                                                          w_cb[:, g:g + 1], ALU.mult, ALU.add), ev[g, 3], z0, wa)
                for j in range(1, 4):
                    m = dve.do(lambda e, g=g, j=j: e.scalar_tensor_tensor(
                        out=cv[:, g, :], in0=xin[:, g, j:j + T], scalar=w_cv[:, g, j:j + 1], in1=cv[:, g, :],
                        op0=ALU.mult, op1=ALU.add), m)
                mu.append(act.do(lambda e, g=g: e.activation(u[:, g, :], cv[:, g, :], ACT.Silu), m))
            row = arena[:, 2048:4096]
            ms = []
            for q in range(4):
                k = 2 + q
                for g in range(2):
                    t = mm(bank(k)[0:33, :], w_xp[:, g, :], u[:, g, 512 * q:512 * q + 512], g == 0, g == 1,
                           mu[g], free[k], sig=(g == 1))
                ms.append(act.do(lambda e, q=q, k=k: e.activation(row[0:33, 512 * q:512 * q + 512],
                                                                  bank(k)[0:33, :], ACT.Copy), t))
                free[k] = ms[-1]
            r1, r2 = arena[0:32, 4096:6144], arena[0:32, 8192:10240]
            m3 = split3(None, row[0:32, :], [ssm3[32 * k:32 * k + 32, :] for k in range(3)], r1, r2, ms[-1], mu[1])
            va, ya, pa = (arena[:, o:o + T] for o in (10240, 12288, 14336))
            mdu = []
            m = None
            for g in range(2):
                for q in range(4):
                    k = 2 + q
                    s = slice(512 * q, 512 * q + 512)
                    t = mm(bank(k), w_dt[32:33, 128 * g:128 * g + 128], row[32:33, s], True, True, ms[-1], free[k],
                           sig=True)
                    v1 = act.do(lambda e, s=s, k=k, g=g: e.activation(va[:, s], bank(k), ACT.Identity,
                                                                      bias=w_db[:, g:g + 1]), t, m, mu[1])
                    v2 = act.do(lambda e, s=s, k=k, g=g: e.activation(ya[:, s], bank(k), ACT.Abs,
                                                                      bias=w_db[:, g:g + 1]), t)
                    free[k] = v2
                v2 = act.do(lambda e: e.activation(ya[:, :], ya[:, :], ACT.Exp, scale=-1.0), v2)
                m = dve.do(lambda e: e.tensor_scalar(pa[:, :], ya[:, :], LOG1P[-1], None, ALU.mult), v2)
                for c in LOG1P[-2::-1]:
                    m = dve.do(lambda e, c=c: e.scalar_tensor_tensor(out=pa[:, :], in0=pa[:, :], scalar=c,
                                                                     in1=ya[:, :], op0=ALU.add, op1=ALU.mult), m)
                m = dve.do(lambda e, g=g: e.scalar_tensor_tensor(out=dl[:, g, :], in0=va[:, :], scalar=0.0,
                                                                 in1=pa[:, :], op0=ALU.max, op1=ALU.add), m)
                mdu.append(pool.do(lambda e, g=g: e.tensor_tensor(du[:, g, :], dl[:, g, :], u[:, g, :], ALU.mult),
                                   m, mu[g]))
            meet()
            NR = 3
            Bb = [arena[:, 1024 * i:1024 * i + TQ] for i in range(2)]
            Cb = [arena[:, 2048 + 1024 * i:2048 + 1024 * i + TQ] for i in range(2)]
            ab, rb, wb, pb = ([arena[:, 4096 + 1024 * (4 * i + j):4096 + 1024 * (4 * i + j) + TQ] for i in range(NR)]
                              for j in range(4))
            rz = [pool.do(lambda e, i=i: e.memset(rb[i], 0.0)) for i in range(NR)]
            freeB, freeC = [None, None], [None, None]
            fr = [dict(a=None, w=None, p=None, r=None) for _ in range(NR)]
            bfree = [None, None]
            yev = None
            hm = {}
            k = 0
            mfin = []
            for tc in range(T // TQ):
                ts = slice(TQ * tc, TQ * tc + TQ)
                ym = None
                for n in range(16):
                    i = n % 2
                    for w, (dst, row_, fz) in enumerate(((Bb, n, freeB), (Cb, 16 + n, freeC))):
                        b0 = 4 + 2 * w
                        for q in range(2):
                            t = mm(bank(b0 + q), sel[:, row_, :], ssm3[:, TQ * tc + 512 * q:TQ * tc + 512 * q + 512],
                                   True, True, bfree[w], m3, c_sel, sig=True)
                        bfree[w] = act.do(lambda e, d=dst[i], b0=b0: e.activation(d, bank(b0, 2), ACT.Copy), t, fz[i])
                    mB, mC = bfree
                    for g in range(2):
                        f = fr[k % NR]
                        a, r, w_, p = ab[k % NR], rb[k % NR], wb[k % NR], pb[k % NR]
                        c = 16 * g + n
                        m_a = act.do(lambda e, a=a, g=g, ts=ts, c=c: e.activation(a, dl[:, g, ts], ACT.Exp,
                                                                                  scale=Am[:, c:c + 1]), f["a"])
                        m_w = pool.do(lambda e, w_=w_, g=g, ts=ts, i=i: e.tensor_tensor(w_, du[:, g, ts], Bb[i],
                                                                                        ALU.mult), mB, f["w"])
                        m_a = dve.do(lambda e, a=a: e.tensor_scalar(a, a, 1.0, 1e-8, ALU.min, ALU.max), m_a)
                        m_r = act.do(lambda e, a=a, r=r: e.mul(r[:, 0:TQ:32], a[:, 0:TQ:32], E20), m_a, f["r"],
                                     rz[-1])
                        m_p = dve.do(lambda e, p=p, a=a, r=r: e.tensor_tensor_scan(
                            out=p, data0=a, data1=r, initial=0.0, op0=ALU.mult, op1=ALU.max), m_r, f["p"])
                        f["r"] = m_p
                        m_w = dve.do(lambda e, p=p, w_=w_: e.scalar_tensor_tensor(
                            out=w_, in0=p, scalar=1.0, in1=w_, op0=ALU.min, op1=ALU.mult), m_p, m_w)
                        freeB[i] = m_w
                        init = 0.0 if tc == 0 else hl[:, c:c + 1]
                        m_x = dve.do(lambda e, p=p, a=a, w_=w_, init=init: e.tensor_tensor_scan(
                            out=p, data0=a, data1=w_, initial=init, op0=ALU.mult, op1=ALU.add), m_w,
                            hm.get(c))
                        f["a"] = m_x
                        if tc < T // TQ - 1:
                            hm[c] = pool.do(lambda e, p=p, c=c: e.tensor_copy(hl[:, c:c + 1], p[:, TQ - 1:TQ]), m_x)
                        m_c = pool.do(lambda e, p=p, w_=w_, i=i: e.tensor_tensor(w_, p, Cb[i], ALU.mult), m_x, mC)
                        f["p"] = m_c
                        freeC[i] = m_c
                        for q in range(2):
                            t = mm(bank(2 * g + q), ident[:, :], w_[:, 512 * q:512 * q + 512], n == 0, n == 15,
                                   m_c, yev, sig=True)
                        f["w"] = t
                        k += 1
                for g in range(2):
                    m = dve.do(lambda e, g=g, ts=ts: e.scalar_tensor_tensor(
                        out=u[:, g, ts], in0=u[:, g, ts], scalar=w_D[:, g:g + 1], in1=bank(2 * g, 2),
                        op0=ALU.mult, op1=ALU.add), t)
                    yev = m
                    m = dve.do(lambda e, g=g, ts=ts: e.tensor_tensor(u[:, g, ts], u[:, g, ts], zs[:, g, ts],
                                                                     ALU.mult), m)
                mfin.append(m)
            meet()
            fz = [None, None]
            for q in range(4):
                b = 4 + q % 2
                for j in range(4):
                    tb = slice(512 * q + 128 * j, 512 * q + 128 * j + 128)
                    for g in range(2):
                        t = mm(bank(b)[:, 128 * j:128 * j + 128], u[:, g, tb], w_out[:, g, :], g == 0, g == 1,
                               fz[q % 2], sig=True)
                xs = x_tok[:, 4 * q:4 * q + 4, :].rearrange("p b d -> p (b d)")
                fz[q % 2] = dve.do(lambda e, xs=xs, b=b: e.tensor_tensor(xs, xs, bank(b), ALU.add), t)
            meet()

        def moe(W1, W2, gates3, xin_marks, nexp, h, hg, hid, bias, acc_extra, wmark):
            hb = [h[:, 0, :], h[:, 1, :], h[:, 2, :]]
            gb = [hg[:, 0, :], hg[:, 1, :], hg[:, 2, :]]
            fh, fg, fu, fG, fo = [None] * 3, [None] * 3, [None] * 3, [None] * 2, [None, None]
            ftr = [None]
            i = 0
            gi = 0
            for q in range(4):
                s = slice(512 * q, 512 * q + 512)
                ob = 6
                steps = [(e_, j) for e_ in range(nexp) for j in range(4)]
                pend = []
                gm = None
                for n, (e_, j) in enumerate(steps):
                    row_ = hid["rows"][e_]
                    if j == 0 and row_ is not None:
                        gbk = 3 + gi % 2
                        gm = mm(bank(gbk), sel[:, row_, :], gates3[:, s], True, True, fG[gi % 2], *xin_marks, sig=True)
                        gcur = gi % 2
                        gi += 1
                    k = i % 3
                    t = mm(bank(k), W1(e_, j), XN[:, s], True, True, fu[k], wmark, *xin_marks, sig=True)
                    m = act.do(lambda e, k=k, f=hid["f"], b=bias(e_, j): e.activation(hb[k], bank(k), f, bias=b),
                               t, fh[k])
                    fu[k] = m
                    if row_ is None:
                        src, owner = hb[k], fh
                    else:
                        m = dve.do(lambda e, k=k, gk=3 + gcur: e.tensor_tensor(gb[k], hb[k], bank(gk), ALU.mult),
                                   m, gm, fg[k])
                        fh[k] = m
                        fG[gcur] = m
                        src, owner = gb[k], fg
                    pend.append((n, e_, j, k, src, owner, m))
                    i += 1
                    if len(pend) > 2 or n == len(steps) - 1:
                        while len(pend) > (0 if n == len(steps) - 1 else 2):
                            n_, e2, j2, k2, src2, own2, m2 = pend.pop(0)
                            last = n_ == len(steps) - 1
                            t = mm(bank(ob), W2(e2, j2), src2, n_ == 0, last and acc_extra is None, m2, fo[0],
                                   sig=True)
                            own2[k2] = t
                            tl = t
                if acc_extra is not None:
                    tl = acc_extra(bank(ob), s)
                ev_ = act.do(lambda e: e.activation(hid["o"], bank(ob), ACT.Copy), tl, ftr[0])
                fo[0] = ev_
                for j in range(4):
                    tt = pe.do(lambda e, j=j: e.transpose(bank(7)[:, 128 * j:128 * j + 128],
                                                          hid["o"][:, 128 * j:128 * j + 128], ident[:, :]),
                               ev_, fo[1])
                ftr[0] = tt
                xs = x_tok[:, 4 * q:4 * q + 4, :].rearrange("p b d -> p (b d)")
                fo[1] = dve.do(lambda e, xs=xs: e.tensor_tensor(xs, xs, bank(7), ALU.add), tt)
                hid["done"](q, fo[1])

        def spread(G, gT, g3, r1, r2, zero, *marks):
            f = [None, None]
            ms = []
            for q in range(4):
                for b in range(4):
                    t = pe.do(lambda e, b=b, q=q: e.transpose(bank(q % 2)[0:8, 128 * b:128 * b + 128],
                                                              G[:, 4 * q + b, :], ident[:, :]), f[q % 2], *marks)
                f[q % 2] = act.do(lambda e, q=q: e.activation(gT[0:8, 512 * q:512 * q + 512], bank(q % 2)[0:8, :],
                                                              ACT.Copy), t)
                ms.append(f[q % 2])
            return split3(None, gT[0:8, :], [g3[32 * k:32 * k + 8, :] for k in range(3)], r1[0:8, :], r2[0:8, :],
                          ms[-1], zero)

        def stage2(ph):
            def sa(name, shape, dt=F32):
                return sb(name, shape, dt, ph)

            f_w1 = sa("f_w1", [128, 9, 512])
            f_w2 = sa("f_w2", [128, 9, 4, 128])
            f_g = sa("f_g", [128, 8])
            lg = sa("lg", [128, NB, 8])
            oh = sa("oh", [128, NB, 8])
            tmp = sa("tmp", [128, NB, 8])
            rank = sa("rank", [128, NB, 8])
            G = sa("G", [128, NB, 8])
            mx = sa("mx", [128, 4, NB])
            g3 = sa("g3", [96, T], BF16)
            ar = sa("ar", [128, 10240])
            d_f.start(sp, f_w1[:, 0, :], A["L0_ffn_shared_w1"])
            d_f.start(sp, f_w1[:, 1:9, :], A["L0_ffn_experts_w1"].rearrange("e d h -> d e h"))
            d_f.start(act, f_w2[:, 0, :, :], A["L0_ffn_shared_w2"].rearrange("(k p) d -> p k d", p=128))
            for x in range(8):
                d_f.start(act, f_w2[:, 1 + x, :, :],
                          A["L0_ffn_experts_w2"][x].rearrange("(k p) d -> p k d", p=128))
            d_f.start(sp, f_g[:, :], A["L0_ffn_gate_w"])
            wf = d_f.mark()
            xn = ar[:, 0:2048].rearrange("p (b d) -> p b d", b=NB)
            ln = layernorm(xn, [])
            zero = pool.do(lambda e: e.memset(g3[:, :], 0.0))
            rk = None
            for x in range(8):
                rk = pool.do(lambda e, x=x: e.memset(rank[:, :, x], 8.0 - x))
            for b in range(NB):
                t = mm(bank(2)[:, 8 * b:8 * b + 8], XN[:, 128 * b:128 * b + 128], f_g[:, :], True, True, wf, ln[b // 4],
                       sig=True)
            m = dve.do(lambda e: e.tensor_copy(lg[:, :, :].rearrange("p b x -> p (b x)"), bank(2)[:, 0:128]), t)

            def bc(v):
                return v.unsqueeze(2).to_broadcast([128, NB, 8])

            def first_max(src, mv_, onehot, m):
                m = dve.do(lambda e: e.tensor_reduce(mv_, src, AX.X, ALU.max), m)
                m = dve.do(lambda e: e.tensor_tensor(tmp[:, :, :], src, bc(mv_), ALU.is_equal), m)
                m = dve.do(lambda e: e.tensor_tensor(tmp[:, :, :], tmp[:, :, :], rank[:, :, :], ALU.mult), m, rk)
                m = dve.do(lambda e: e.tensor_reduce(mx[:, 2, :], tmp[:, :, :], AX.X, ALU.max), m)
                return dve.do(lambda e: e.tensor_tensor(onehot, tmp[:, :, :], bc(mx[:, 2, :]), ALU.is_equal), m)

            m = first_max(lg[:, :, :], mx[:, 0, :], oh[:, :, :], m)
            m = dve.do(lambda e: e.scalar_tensor_tensor(out=lg[:, :, :], in0=oh[:, :, :], scalar=-3.0e38,
                                                        in1=lg[:, :, :], op0=ALU.mult, op1=ALU.add), m)
            m = first_max(lg[:, :, :], mx[:, 1, :], G[:, :, :], m)
            m = dve.do(lambda e: e.tensor_tensor(mx[:, 2, :], mx[:, 1, :], mx[:, 0, :], ALU.subtract), m)
            m = act.do(lambda e: e.activation(mx[:, 2, :], mx[:, 2, :], ACT.Exp), m)
            m = dve.do(lambda e: e.tensor_scalar(mx[:, 3, :], mx[:, 2, :], 1.0, None, ALU.add), m)
            m = dve.do(lambda e: e.reciprocal(mx[:, 3, :], mx[:, 3, :]), m)
            m = dve.do(lambda e: e.tensor_tensor(mx[:, 2, :], mx[:, 2, :], mx[:, 3, :], ALU.mult), m)
            m = dve.do(lambda e: e.tensor_tensor(oh[:, :, :], oh[:, :, :], bc(mx[:, 3, :]), ALU.mult), m)
            m = dve.do(lambda e: e.tensor_tensor(G[:, :, :], G[:, :, :], bc(mx[:, 2, :]), ALU.mult), m)
            m = dve.do(lambda e: e.tensor_tensor(G[:, :, :], G[:, :, :], oh[:, :, :], ALU.add), m)
            mg = spread(G, ar[:, 2048:4096], g3, ar[:, 4096:6144], ar[:, 6144:8192], zero, m)
            meet()
            h = ar[:, 0:1536].rearrange("p (a b) -> p a b", a=3)
            hg = ar[:, 1536:3072].rearrange("p (a b) -> p a b", a=3)
            hid = dict(rows=[None] + list(range(8)), f=ACT.Silu, o=ar[:, 3072:3584], done=lambda q, m: None)
            moe(lambda e_, j: f_w1[:, e_, 128 * j:128 * j + 128], lambda e_, j: f_w2[:, e_, j, :], g3, [mg], 9,
                h, hg, hid, lambda e_, j: 0.0, None, wf)
            meet()

        def stage3(ph):
            def sa(name, shape, dt=F32):
                return sb(name, shape, dt, ph)

            d_w = loads("d_w")
            W = {}
            for nm in ("Wq", "Wk", "Wv", "out"):
                W[nm] = sa("w_" + nm + "1", [128, 128])
                d_w.start(sp, W[nm][:, :], A[f"L1_attn_{nm}_w"])
            for nm in ("convq", "convk"):
                W[nm] = sa("w_" + nm, [128, 3, 128])
                d_w.start(sp, W[nm][:, :, :], A[f"L1_attn_{nm}_w"])
            for nm in ("qproj", "kproj"):
                W[nm] = sa("w_" + nm, [128, 2, 128])
                d_w.start(sp, W[nm][:, :, :], A[f"L1_attn_{nm}_w"].rearrange("(g p) n -> p g n", p=128))
            cols = sa("cols", [128, 8])
            d_w.start(sp, cols[:, :], A["cols"])
            t1w = sa("t1w", [128, 2, 2, 4])
            d_w.start(sp, t1w[:, :, :, :], A["t1w"])
            t2w = sa("t2w", [128, 2, 128])
            d2w = sa("d2w", [128, 2, 16])
            d_w.start(sp, t2w[:, :, :], A["L1_attn_tau2_w"].rearrange("(p g) n -> p g n", g=2))
            d_w.start(sp, d2w[:, :, :], A["L1_attn_del2_w"].rearrange("(p g) n -> p g n", g=2))
            bb = sa("bb", [128, 2, 128])
            d_w.start(sp, bb[:, 0, :], A["L1_attn_Wv_b"].partition_broadcast(128))
            d_w.start(sp, bb[:, 1, :], A["L1_attn_out_b"].partition_broadcast(128))
            ww = d_w.mark()

            tauR = sa("tauR", [128, T])
            va = sa("va", [128, NB, NH, 32])
            QZ = sa("QZ", [128, 2, NH, 512], BF16)
            tmpl = sa("tmpl", [128, NH])
            KS = sa("KS", [128, 8, T], BF16)
            aa = sa("aa", [128, 12288])

            zq = dve.do(lambda e: e.memset(va[:, :, :, :], 0.0))
            zq = dve.do(lambda e: e.memset(va[:, :, :, 8:9], 1.0), zq)
            z2 = dve.do(lambda e: e.memset(KS[:, :, :].bitcast(mybir.dt.uint32), 0x3F803F80))
            z1 = pool.do(lambda e: e.memset(tmpl[:, :], 1.0))
            for hh in range(2):
                tv = tmpl[:, hh:NH:2]
                z1 = pool.do(lambda e, tv=tv, hh=hh: e.affine_select(
                    out=tv, in_=tv, compare_op=ALU.is_ge, fill=0.0, base=-(64 * hh + 48), pattern=[[0, 8]],
                    channel_multiplier=1), z1)
                z1 = pool.do(lambda e, tv=tv, hh=hh: e.affine_select(
                    out=tv, in_=tv, compare_op=ALU.is_ge, fill=0.0, base=64 * hh + 50, pattern=[[0, 8]],
                    channel_multiplier=-1), z1)
            zb = [pool.do(lambda e, i=i: e.tensor_copy(QZ[:, i, :, :],
                                                       tmpl[:, :].unsqueeze(2).to_broadcast([128, NH, 512])), z1)
                  for i in range(2)]
            zrow = sa("zrow", [3, 8, 512], BF16)
            zz = pool.do(lambda e: e.memset(zrow[:, :, :], 0.0))
            ln = layernorm(aa[:, 0:2048].rearrange("p (b d) -> p b d", b=NB), [])
            delT = aa[0:16, 10240:12288]
            free = [None] * 8
            prev = []
            mm_tau = None
            for i in range(2):
                gl = []
                for g in range(2):
                    cvt = aa[:, 2048 + 2048 * g:4096 + 2048 * g]
                    m = dve.do(lambda e, i=i, g=g, c=cvt: e.tensor_scalar(
                        c, xnT[:, 0:T], t1w[:, i, g, 0:1], t1w[:, i, g, 3:4], ALU.mult, ALU.add), ww, ln[3], *prev)
                    for j in (1, 2):
                        m = dve.do(lambda e, i=i, g=g, j=j, c=cvt: e.scalar_tensor_tensor(
                            out=c, in0=xnT[:, j:j + T], scalar=t1w[:, i, g, j:j + 1], in1=c,
                            op0=ALU.mult, op1=ALU.add), m)
                    gl.append(act.do(lambda e, c=cvt: e.activation(c, c, ACT.Gelu), m))
                prev = []
                for q in range(4):
                    s = slice(512 * q, 512 * q + 512)
                    k = 2 + q
                    w2, o, bcol, M = ((t2w, tauR, cols[:, 6:7], 128), (d2w, delT, cols[0:16, 7:8], 16))[i]
                    for g in range(2):
                        t = mm(bank(k)[0:M, :], w2[:, g, :], aa[:, 2048 + 2048 * g + 512 * q:2560 + 2048 * g + 512 * q],
                               g == 0, g == 1, gl[g], free[k], ww, sig=True)
                    prev.append(t)
                    free[k] = act.do(lambda e, o=o, s=s, k=k, M=M, bcol=bcol: e.activation(
                        o[:, s], bank(k)[0:M, :], ACT.Sigmoid, bias=bcol), t)
                    last = free[k]
            mtau = last
            sc = scratch("sc", [7, 128, T], BF16)
            d_s = loads("d_s")
            rr1, rr2 = aa[:, 6144:8192], aa[:, 8192:10240]
            parts = aa[:, 0:3072].bitcast(BF16).rearrange("p (k t) -> p k t", k=3)
            m = split3(None, delT, [parts[0:16, k, :] for k in range(3)], rr1[0:16, :], rr2[0:16, :], last, *prev)
            d_r = loads("d_r")
            for hh in range(2):
                for k in range(3):
                    src = parts[0:16, k, :]
                    d_s.start(sp, sc[6, 16 * k:16 * k + 16, :], src, m) if hh == 0 else None
            mds = d_s.mark()
            for hh in range(2):
                for k in range(3):
                    srcd = sc[6, 16 * k:16 * k + 16, :].rearrange("(a b) t -> b a t", b=2)[hh:hh + 1, :, :]
                    d_r.start(sp, KS[64 * hh + 48 + k:64 * hh + 49 + k, :, :], srcd, mds, z2)
            grp = ([0, 1, 0, 1, 2, 0], [0, 0, 1, 1, 0, 2])
            pd = aa[:, 0:T + 2]
            mprev = [mds, m]
            for i, (wn, cn, pn) in enumerate((("Wq", "convq", "qproj"), ("Wk", "convk", "kproj"))):
                pd = aa[:, 3072:3072 + T + 2]
                c3 = aa[:, 5200:5200 + T]
                qv = aa[:, 7300:7300 + T]
                sr = aa[:, 9400:9400 + T]
                z = [dve.do(lambda e: e.memset(pd[:, 0:1], 0.0), *mprev),
                     dve.do(lambda e: e.memset(pd[:, T + 1:T + 2], 0.0), *mprev)]
                ev_ = []
                for q in range(4):
                    k = 2 + q
                    t = mm(bank(k), W[wn][:, :], XN[:, 512 * q:512 * q + 512], True, True, free[k], sig=True)
                    free[k] = act.do(lambda e, k=k, q=q, i=i: e.activation(
                        pd[:, 1 + 512 * q:513 + 512 * q], bank(k), ACT.Identity, bias=cols[:, i:i + 1]), t, z)
                    ev_.append(free[k])
                ev2 = []
                for q in range(4):
                    k = 2 + q
                    for j in range(3):
                        t = mm(bank(k), W[cn][:, j, :], pd[:, 512 * q + j:512 * q + j + 512], j == 0, j == 2,
                               free[k], ev_, sig=(j == 2))
                    free[k] = act.do(lambda e, k=k, q=q, i=i: e.activation(
                        c3[:, 512 * q:512 * q + 512], bank(k), ACT.Identity, bias=cols[:, 2 + i:3 + i]), t)
                    ev2.append(free[k])
                ev3 = []
                for q in range(4):
                    k = 2 + q
                    mm(bank(k), W[pn][:, 0, :], pd[:, 1 + 512 * q:513 + 512 * q], True, False, free[k], ev2)
                    t = mm(bank(k), W[pn][:, 1, :], c3[:, 512 * q:512 * q + 512], False, True, sig=True)
                    free[k] = act.do(lambda e, k=k, q=q, i=i: e.activation(
                        qv[:, 512 * q:512 * q + 512], bank(k), ACT.Identity, bias=cols[:, 4 + i:5 + i]), t)
                    ev3.append(free[k])
                m = ev3[-1]
                if i == 0:
                    m = dve.do(lambda e: e.scalar_tensor_tensor(out=qv, in0=qv, scalar=float(8.0 ** -0.5),
                                                                in1=tauR[:, :], op0=ALU.mult, op1=ALU.mult), m, mtau)
                mprev2 = split3(None, qv, [parts[:, k, :] for k in range(3)], c3, sr, m, *mprev, t)
                for k in range(3):
                    d_s.start(sp, sc[3 * i + k, :, :], parts[:, k, :], mprev2)
                mds = d_s.mark()
                mprev = [mds, mprev2]
                for hh in range(2 if i else 0):
                    for gi, pk in enumerate(grp[i]):
                        srcd = sc[3 * i + pk].rearrange("(a b r) t -> b r a t", b=2, r=8)[hh]
                        d_r.start(sp, KS[64 * hh + 8 * gi:64 * hh + 8 * gi + 8, :, :], srcd, mds, z2)
            mqk = d_r.mark()
            for q in range(4):
                k = 2 + q
                for b in range(4):
                    tb = 4 * q + b
                    t = mm(bank(k)[:, 128 * b:128 * b + 128], XN[:, 128 * tb:128 * tb + 128], W["Wv"][:, :],
                           True, True, free[k], sig=True)
                for b in range(4):
                    tb = 4 * q + b
                    m = dve.do(lambda e, k=k, b=b, tb=tb: e.tensor_tensor(
                        va[:, tb, :, 0:8], bank(k)[:, 128 * b:128 * b + 128].rearrange("p (h r) -> p h r", h=16),
                        bb[:, 0, :].rearrange("p (h r) -> p h r", h=16), ALU.add), t, zq)
                free[k] = m
            mva = m
            meet()
            NG = 16
            Pt = [aa[:, 2048 * i:2048 * i + 2048] for i in range(3)]
            Oe = aa[:, 6144:6656]
            nm = aa[0:4, 6656:7168]
            n1, n2 = aa[0:4, 7168:7680], aa[0:4, 7680:8192]
            n3 = aa[0:4, 8192:8960].bitcast(BF16).rearrange("p (k t) -> p k t", k=3)
            rs = aa[:, 8960:8976]
            mx4 = aa[:, 9024:9024 + 64].rearrange("p (b h c) -> p b h c", b=4, h=4)
            mxh = aa[:, 9088:9104].rearrange("p (b h) -> p b h", b=4)
            at = aa[:, 9216:9728].rearrange("p (b d) -> p b d", b=4)
            att = aa[:, 9728:10240]
            fS = [None, None]
            fP = [None] * 3
            fM = [None, None]
            fO = [None, None]
            stt = dict(n3=None, mxh=None, nm=None, at=None, att=None, oe=None, last=None)
            d_q = [loads(f"d_q{i}") for i in range(2)]
            d_n = loads("d_n")
            d_m = loads("d_m")
            used = [None, None]
            mrow = {}
            qkm = {}

            def load_q(qc):
                sl = qc % 2
                qs = slice(512 * qc, 512 * qc + 512)
                for hh in range(2):
                    for gi, pk in enumerate(grp[0]):
                        srcd = sc[pk, :, qs].rearrange("(a b r) t -> b r a t", b=2, r=8)[hh]
                        d_q[sl].start(sp, QZ[64 * hh + 8 * gi:64 * hh + 8 * gi + 8, sl, hh:NH:2, :], srcd, mqk, zb,
                                      used[sl])
                    if qc >= 2:
                        d_q[sl].start(sp, QZ[64 * hh + 51:64 * hh + 54, sl, hh:NH:2, :], zrow[:, :, :], zz, used[sl])
                qkm[qc] = d_q[sl].mark()

            def maxima(G):
                qc, hg = divmod(G, 4)
                cnt = 0
                for b in range(4):
                    for hl_ in range(4):
                        h = 4 * hg + hl_
                        for c in range(4):
                            k = cnt % 2
                            cnt += 1
                            t = mm(bank(4 + k), QZ[:, qc % 2, h, 128 * b:128 * b + 128],
                                   KS[:, h // 2, 512 * c:512 * c + 512], True, True, fM[k], mqk, qkm[qc], sig=True)
                            fM[k] = dve.do(lambda e, b=b, hl_=hl_, c=c, k=k: e.tensor_reduce(
                                mx4[:, b, hl_, c:c + 1], bank(4 + k), AX.X, ALU.max), t, stt["mxh"])
                            yield
                m = dve.do(lambda e: e.tensor_reduce(mxh, mx4, AX.X, ALU.max, negate=True), fM[0], fM[1], stt["nm"])
                stt["mxh"] = m
                yield
                for b in range(4):
                    t = pe.do(lambda e, b=b: e.transpose(bank(4)[0:4, 128 * b:128 * b + 128], mxh[:, b, :],
                                                         ident[:, :]), m, fM[0])
                stt["nm"] = t
                m = act.do(lambda e: e.activation(nm, bank(4)[0:4, :], ACT.Copy), t, stt["n3"])
                fM[0] = m
                yield
                m0 = pool.do(lambda e: e.tensor_copy(n3[:, 0, :], nm), m, d_n.mark() if G else None)
                m = pool.do(lambda e: e.tensor_tensor(n1, nm, n3[:, 0, :], ALU.subtract), m0)
                m = pool.do(lambda e: e.tensor_copy(n3[:, 1, :], n1), m)
                m = pool.do(lambda e: e.tensor_tensor(n2, n1, n3[:, 1, :], ALU.subtract), m)
                m = pool.do(lambda e: e.tensor_copy(n3[:, 2, :], n2), m)
                stt["n3"] = m
                qs = slice(512 * qc, 512 * qc + 512)
                nd = sc[6, 48:96, qs].rearrange("(k g h) t -> g h k t", k=3, g=4)[hg]
                d_n.start(sp, nd, n3, m)
                for hh in range(2):
                    srcd = sc[6, 48:96, qs].rearrange("(k g a b) t -> g b k a t", k=3, g=4, b=2)[hg, hh]
                    d_m.start(sp, QZ[64 * hh + 51:64 * hh + 54, qc % 2, 4 * hg + hh:4 * hg + 4:2, :], srcd,
                              d_n.mark(), stt["nm"])
                mrow[G] = d_m.mark()
                yield

            def outputs(G, tl):
                qc, hg = divmod(G, 4)
                ob = bank(6 + G % 2)
                m = dve.do(lambda e: e.tensor_copy(Oe, ob), tl, stt["oe"])
                yield
                for b in range(4):
                    tt = pe.do(lambda e, b=b: e.transpose(ob[:, 128 * b:128 * b + 128], Oe[:, 128 * b:128 * b + 128],
                                                          ident[:, :]), m)
                stt["oe"] = tt
                yield
                v7 = ob.rearrange("p (b h c) -> p b h c", b=4, h=4)
                rv = rs.rearrange("p (b h o) -> p b h o", b=4, h=4)
                m = dve.do(lambda e: e.reciprocal(rv, v7[:, :, :, 8:9]), tt)
                for b in range(4):
                    m2 = dve.do(lambda e, b=b: e.tensor_tensor(
                        at[:, b, 32 * hg:32 * hg + 32].rearrange("p (h r) -> p h r", h=4),
                        v7[:, b, :, 0:8], rv[:, b, :, :].to_broadcast([128, 4, 8]), ALU.mult), m, stt["at"])
                fO[G % 2] = m2
                yield
                if hg == 3:
                    for b in range(4):
                        tt = pe.do(lambda e, b=b: e.transpose(ob[:, 128 * b:128 * b + 128], at[:, b, :],
                                                              ident[:, :]), m2)
                    stt["at"] = tt
                    yield
                    m = act.do(lambda e: e.activation(att, ob, ACT.Copy), tt, stt["att"])
                    yield
                    for b in range(4):
                        t = mm(ob[:, 128 * b:128 * b + 128], att[:, 128 * b:128 * b + 128], W["out"][:, :],
                               True, True, m, sig=True)
                    stt["att"] = t
                    yield
                    xs = x_tok[:, 4 * qc:4 * qc + 4, :]
                    b7 = ob.rearrange("p (b d) -> p b d", b=4)
                    m = dve.do(lambda e: e.tensor_tensor(xs, xs, b7, ALU.add), t)
                    fO[G % 2] = m
                    m = dve.do(lambda e: e.tensor_tensor(xs, xs, bb[:, 1:2, :].to_broadcast([128, 4, 128]), ALU.add),
                               m)
                    yield

            def pull(gen, n=1):
                for _ in range(n):
                    if gen is not None and next(gen, 0) == 0:
                        return None
                return gen

            def all_maxima():
                for G in range(NG):
                    if G == 0:
                        load_q(0)
                    if G % 4 == 2 and G < 14:
                        load_q(G // 4 + 1)
                    yield from maxima(G)

            gen = all_maxima()
            gen = pull(gen, 67 + 26)
            post = None
            for G in range(NG):
                qc, hg = divmod(G, 4)

                def pv(kb, pt, ms):
                    for j in range(4):
                        f = pe.do if j == 3 else pe.quiet
                        t = f(lambda e, j=j, kb=kb, pt=pt, hg=hg, G=G: e.matmul(
                            bank(6 + G % 2)[32 * j:32 * j + 32, :], va[:, kb, 4 * hg + j, :],
                            pt[:, 512 * j:512 * j + 512], start=(kb == 0), stop=(kb == NB - 1)),
                            ms, fO[G % 2] if kb == 0 else None, mva)
                    return t

                pend = None
                for kb in range(NB):
                    pt = Pt[kb % 3]
                    ms = []
                    for pp in range(2):
                        for hh in range(2):
                            h = 4 * hg + 2 * pp + hh
                            t = mm(bank(2 * pp + hh), KS[:, h // 2, 128 * kb:128 * kb + 128],
                                   QZ[:, qc % 2, h, :], True, True, fS[pp], mrow[G], sig=(hh == 1))
                        m = act.do(lambda e, pt=pt, pp=pp: e.activation(pt[:, 1024 * pp:1024 * pp + 1024],
                                                                        bank(2 * pp, 2), ACT.Exp), t, fP[kb % 3])
                        fS[pp] = m
                        ms.append(m)
                        gen = pull(gen, 1)
                    if pend is not None:
                        fP[(kb - 1) % 3] = pv(*pend)
                    pend = (kb, pt, ms)
                    gen = pull(gen, 2 + (kb % 4 == 1))
                    if kb >= 1:
                        post = pull(post)
                fP[(NB - 1) % 3] = tl = pv(*pend)
                while post is not None:
                    post = pull(post)
                used[qc % 2] = tl
                post = outputs(G, tl)
            while post is not None:
                post = pull(post)
            meet()

        def stage4(ph):
            def sa(name, shape, dt=F32):
                return sb(name, shape, dt, ph)

            d_g = loads("d_g")
            h_w1 = sa("h_w1", [128, 8, 512])
            h_w2 = sa("h_w2", [128, 8, 4, 128])
            h_b1 = sa("h_b1", [128, 8, 4])
            h_b2 = sa("h_b2", [8, 128])
            d_g.start(sp, h_w1[:, :, :], A["L1_ffn_W1"].rearrange("e d h -> d e h"))
            for x in range(8):
                d_g.start(sp, h_w2[:, x, :, :], A["L1_ffn_W2"][x].rearrange("(k p) d -> p k d", p=128))
            d_g.start(sp, h_b1[:, :, :], A["L1_ffn_b1"])
            d_g.start(sp, h_b2[:, :], A["L1_ffn_b2"])
            wg = d_g.mark()
            ar = sa("ar2", [128, 10240])
            g3 = sa("g32", [96, T], BF16)
            kk = sa("kk", [128, NB, 16])
            c16 = sa("c16", [128, NB, 16])
            sv = sa("sv", [128, 4, NB])
            eA = sa("eA", [128, 2, NB, 8])
            G = sa("Gh", [128, NB, 8])
            G2 = sa("Gh2", [128, NB, 8])
            xn = ar[:, 0:2048].rearrange("p (b d) -> p b d", b=NB)
            cm = None
            for x in range(16):
                cm = pool.do(lambda e, x=x: e.memset(kk[:, :, x], float(x + 1)))
            for x in range(8):
                cm = pool.do(lambda e, x=x: e.memset(eA[:, 0, :, x], float(x)))
                cm = pool.do(lambda e, x=x: e.memset(eA[:, 1, :, x], float((x + 7) % 8)))
            zero = pool.do(lambda e: e.memset(g3[:, :], 0.0))
            ln = layernorm(xn, [])
            s_, tr, a_, b_ = (sv[:, i, :] for i in range(4))
            m = dve.do(lambda e: e.tensor_tensor(s_, xn[:, :, 0], xn[:, :, 1], ALU.add), ln[3])

            def count(dst, src, op, n, lane_m):
                m = dve.do(lambda e: e.tensor_tensor(c16[:, :, 0:n], src.unsqueeze(2).to_broadcast([128, NB, n]),
                                                     kk[:, :, 0:n], op), lane_m, cm)
                return dve.do(lambda e: e.tensor_reduce(dst, c16[:, :, 0:n], AX.X, ALU.add), m)

            m = count(a_, s_, ALU.is_ge, 16, m)
            m = dve.do(lambda e: e.tensor_scalar(s_, s_, -1.0, None, ALU.mult), m)
            m = count(b_, s_, ALU.is_ge, 16, m)
            m = dve.do(lambda e: e.tensor_tensor(tr, a_, b_, ALU.subtract), m)
            m = dve.do(lambda e: e.tensor_scalar(a_, tr, 16.0, 0.125, ALU.add, ALU.mult), m)
            m = count(b_, a_, ALU.is_ge, 4, m)
            m = dve.do(lambda e: e.scalar_tensor_tensor(out=tr, in0=b_, scalar=-8.0, in1=tr, op0=ALU.mult,
                                                        op1=ALU.add), m)
            m = dve.do(lambda e: e.tensor_scalar(tr, tr, 16.0, None, ALU.add), m)
            hb_ = tr.unsqueeze(2).to_broadcast([128, NB, 8])
            m = dve.do(lambda e: e.tensor_tensor(G[:, :, :], eA[:, 0, :, :], hb_, ALU.is_equal), m)
            m = dve.do(lambda e: e.tensor_tensor(G2[:, :, :], eA[:, 1, :, :], hb_, ALU.is_equal), m)
            m = dve.do(lambda e: e.tensor_tensor(G[:, :, :], G[:, :, :], G2[:, :, :], ALU.add), m)
            m = dve.do(lambda e: e.tensor_scalar(G[:, :, :], G[:, :, :], 0.5, None, ALU.mult), m)
            gT = ar[:, 8192:10240]
            mg = spread(G, gT, g3, ar[:, 4096:6144], ar[:, 6144:8192], zero, m)
            meet()
            h = ar[:, 0:1536].rearrange("p (a b) -> p a b", a=3)
            hg = ar[:, 1536:3072].rearrange("p (a b) -> p a b", a=3)
            d_o = loads("d_o")
            ov = out.rearrange("o (b p) d -> p (o b) d", p=128)

            def done(q, m):
                d_o.start(sp, ov[:, 4 * q:4 * q + 4, :], x_tok[:, 4 * q:4 * q + 4, :], m)

            hid = dict(rows=list(range(8)), f=ACT.Relu, o=ar[:, 3072:3584], done=done)
            moe(lambda e_, j: h_w1[:, e_, 128 * j:128 * j + 128], lambda e_, j: h_w2[:, e_, j, :], g3, [mg], 8,
                h, hg, hid, lambda e_, j: h_b1[:, e_, j:j + 1],
                lambda o, s: mm(o, h_b2[:, :], gT[0:8, s], False, True, sig=True), wg)
            sp.wait(d_o.mark())

        for n, stage in enumerate((stage1, stage2, stage3, stage4)):
            with ExitStack() as ph:
                stage(ph)
            if DEBUG == n + 1:
                finish(ctx, nc, lanes, x_tok, out, loads, meet)
                return
        play(ctx, nc, lanes)


def play(ctx, nc, lanes):
    pe, act, dve, pool, sp = lanes
    block = ctx.enter_context(nc.Block())

    @block.tensor
    def _(e):
        pe.play(e)

    @block.scalar
    def _(e):
        act.play(e)

    @block.vector
    def _(e):
        dve.play(e)

    @block.gpsimd
    def _(e):
        pool.play(e)

    @block.sync
    def _(e):
        sp.play(e)


def finish(ctx, nc, lanes, x_tok, out, loads, meet):
    d_o = loads("d_o")
    meet()
    d_o.start(lanes[4], out.rearrange("o (b p) d -> p (o b) d", p=128), x_tok[:, :, :])
    lanes[4].wait(d_o.mark())
    play(ctx, nc, lanes)


DEBUG = 0


def kernel(**inputs):
    import numpy as _np
    import concourse.bacc as _bacc
    from concourse import mybir as _mybir
    from concourse.bass_utils import run_bass_kernel_spmd as _run

    a = {k: _np.asarray(v) for k, v in inputs.items()}
    lay = dict(a)
    for n in ("L0_attn_conv_b", "L0_attn_dt_b", "L0_attn_D_param"):
        lay[n] = a[n].reshape(2, 128).T
    lay["L0_ffn_shared_w1"] = a["L0_ffn_shared_w1"].T
    lay["L0_ffn_shared_w2"] = a["L0_ffn_shared_w2"].T
    lay["L0_ffn_experts_w1"] = a["L0_ffn_experts_w1"].transpose(0, 2, 1)
    lay["L0_ffn_experts_w2"] = a["L0_ffn_experts_w2"].transpose(0, 2, 1)
    lay["L0_ffn_gate_w"] = a["L0_ffn_gate_w"].T
    for n in ("Wq_w", "Wk_w", "Wv_w", "out_w", "qproj_w", "kproj_w"):
        lay["L1_attn_" + n] = a["L1_attn_" + n].T
    for n in ("convq_w", "convk_w"):
        lay["L1_attn_" + n] = a["L1_attn_" + n].transpose(1, 2, 0)
    rep = _np.repeat(a["L1_attn_tau2_b"], 8)
    lay["cols"] = _np.stack([lay.pop("L1_attn_" + n) for n in ("Wq_b", "Wk_b", "convq_b", "convk_b", "qproj_b",
                                                              "kproj_b")]
                            + [rep, _np.pad(lay.pop("L1_attn_del2_b"), (0, 112))], axis=1)
    lay.pop("L1_attn_tau2_b")
    lay["t1w"] = _np.stack([_np.concatenate([lay.pop(f"L1_attn_{n}_w").reshape(128, 2, 3),
                                             lay.pop(f"L1_attn_{n}_b").reshape(128, 2, 1)], axis=2)
                            for n in ("tau1", "del1")], axis=1)
    lay["L1_attn_tau2_w"] = _np.repeat(a["L1_attn_tau2_w"][:, :, 0], 8, axis=0).T
    lay["L1_attn_del2_w"] = a["L1_attn_del2_w"][:, :, 0].T
    lay["L1_ffn_b1"] = a["L1_ffn_b1"].reshape(8, 4, 128).transpose(2, 0, 1)
    nc = _bacc.Bacc("TRN2", target_bir_lowering=False, num_devices=1)
    arrays, aps = {}, {}
    for n, v in lay.items():
        v = _np.ascontiguousarray(v)
        arrays[f"in_{n}"] = v
        aps[n] = nc.dram_tensor(f"in_{n}", v.shape, _mybir.dt.from_np(v.dtype), kind="ExternalInput").ap()
    o = nc.dram_tensor("out_0", (1, 2048, 128), _mybir.dt.float32, kind="ExternalOutput").ap()
    build(nc, aps, o)
    r = _run(nc, [arrays], core_ids=[0])
    return r.results[0]["out_0"]
```

```python
from contextlib import ExitStack

import concourse.bass as bass
import numpy as np
from concourse import mybir

ALU = mybir.AluOpType
ACT = mybir.ActivationFunctionType
AX = mybir.AxisListType
F32 = mybir.dt.float32
BF16 = mybir.dt.bfloat16

T = 2048
NB = T // 128
NH = 16
E20 = float(np.float32(np.exp(20.0)))
LEAD_PULLS = 16
LEAD = 0.002037716592261226
PAIRS = [(2.303017180067723, 0.5212684734404347), (1.7051292196135144, 1.388852113778505),
         (0.7105420929209361, 1.7893626000831488), (-0.34221934465336235, 1.5852768471090855),
         (-1.0774327183153332, 0.8401208583996678)]


class Lane:

    def __init__(self, name, sem):
        self.name, self.sem, self.count, self.seen, self.items = name, sem, 0, {}, []

    def wait(self, *marks):
        for m in marks:
            if m is None:
                continue
            if isinstance(m, list):
                self.wait(*m)
                continue
            sem, value = m
            if self.seen.get(sem.name, 0) < value:
                self.seen[sem.name] = value
                self.items.append(lambda e, s=sem, v=value: e.wait_ge(s, v))

    def do(self, fn, *marks):
        self.wait(*marks)
        self.count += 1
        self.items.append(lambda e, s=self.sem: fn(e).then_inc(s, 1))
        return (self.sem, self.count)

    def quiet(self, fn, *marks):
        self.wait(*marks)
        self.items.append(lambda e: fn(e))

    def play(self, e):
        for item in self.items:
            item(e)


def iter_chain(*gens):
    for g in gens:
        yield from g


class Loads:

    def __init__(self, sem):
        self.sem, self.count = sem, 0

    def start(self, lane, out, in_, *marks):
        lane.wait(*marks)
        self.count += 16
        lane.items.append(lambda e: e.dma_start(out, in_).then_inc(self.sem, 16))

    def mark(self):
        return (self.sem, self.count)


def build(nc, A, out):
    with ExitStack() as ctx:
        def sem(name):
            return ctx.enter_context(nc.semaphore(name))

        pe, act, dve, pool, sp = (Lane(n, sem("s_" + n)) for n in ("pe", "act", "dve", "pool", "sp"))
        lanes = (pe, act, dve, pool, sp)

        def sb(name, shape, dt=F32, stack=ctx):
            return stack.enter_context(nc.sbuf_tensor(name, shape, dt))

        def loads(name):
            return Loads(sem(name))

        def scratch(name, shape, dt):
            return nc.dram_tensor(name, shape, dt, kind="Internal").ap()

        PS = ctx.enter_context(nc.psum_tensor("PS", [128, 8, 512], F32))

        def bank(i, n=1):
            return PS[:, i, :] if n == 1 else PS[:, i:i + n, :].rearrange("p a b -> p (a b)")

        def meet():
            marks = [(x.sem, x.count) for x in lanes if x.count]
            for x in lanes:
                x.wait(*marks)

        x_tok = sb("x_tok", [128, NB, 128])
        xnT = sb("xnT", [128, T + 2])
        XN = xnT[:, 1:T + 1]
        ident = sb("ident", [128, 128])
        identb = sb("identb", [128, 128], BF16)
        cst = sb("cst", [128, 5])
        st6 = sb("st6", [128, NB, 6])
        mv = sb("mv", [128, NB, 2])
        rstd = sb("rstd", [128, NB])
        mhalf = sb("mhalf", [128, NB])

        d_x = loads("d_x")
        d_a = loads("d_a")
        d_f = loads("d_f")
        xv = A["L0_attn_x"].rearrange("o (b p) d -> p (o b) d", p=128)
        d_x.start(sp, x_tok[:, :, :], xv)

        c0 = pool.do(lambda e: e.memset(ident[:, :], 0.0))
        c1 = pool.do(lambda e: e.affine_select(out=ident[:, :], in_=ident[:, :], compare_op=ALU.not_equal, fill=1.0,
                                               base=0, pattern=[[-1, 128]], channel_multiplier=1), c0)
        for i, (re_, _) in enumerate(PAIRS):
            c5 = pool.do(lambda e, i=i, re_=re_: e.memset(cst[:, i:i + 1], -re_))
        c2 = pool.do(lambda e: e.memset(mhalf[:, :], -0.5))
        c3 = dve.do(lambda e: e.memset(xnT[:, 0:1], 0.0))
        c4 = dve.do(lambda e: e.memset(xnT[:, T + 1:T + 2], 0.0))
        c_const = [c1, c2, c3, c4]

        def mm(o, l, r, start, stop, *marks, sig=False):
            f = pe.do if sig else pe.quiet
            return f(lambda e: e.matmul(o, l, r, start=start, stop=stop), *marks)

        W = {nm: sb("w_" + nm + "1", [128, 128]) for nm in ("Wq", "Wk", "Wv", "out")}
        W.update({nm: sb("w_" + nm, [128, 3, 128]) for nm in ("convq", "convk")})
        W.update({nm: sb("w_" + nm, [128, 2, 128]) for nm in ("qproj", "kproj")})
        cols = sb("cols", [128, 8])
        t1w = sb("t1w", [128, 2, 2, 4])
        t2w = sb("t2w", [128, 2, 128])
        d2w = sb("d2w", [128, 2, 16])
        bb = sb("bb", [128, 2, 128])
        d_w = loads("d_w")

        def load_weights():
            for nm in ("Wq", "Wk", "Wv", "out"):
                d_w.start(sp, W[nm][:, :], A[f"L1_attn_{nm}_w"])
            for nm in ("convq", "convk"):
                d_w.start(sp, W[nm][:, :, :], A[f"L1_attn_{nm}_w"])
            for nm in ("qproj", "kproj"):
                d_w.start(sp, W[nm][:, :, :], A[f"L1_attn_{nm}_w"].rearrange("(g p) n -> p g n", p=128))
            d_w.start(sp, cols[:, :], A["cols"])
            d_w.start(sp, t1w[:, :, :, :], A["t1w"])
            d_w.start(sp, t2w[:, :, :], A["L1_attn_tau2_w"].rearrange("(p g) n -> p g n", g=2))
            d_w.start(sp, d2w[:, :, :], A["L1_attn_del2_w"].rearrange("(p g) n -> p g n", g=2))
            d_w.start(sp, bb[:, 0, :], A["L1_attn_Wv_b"].partition_broadcast(128))
            d_w.start(sp, bb[:, 1, :], A["L1_attn_out_b"].partition_broadcast(128))

        def stage1(ph):
            def sa(name, shape, dt=F32):
                return sb(name, shape, dt, ph)

            sel = sa("sel", [96, 32, 128], BF16)
            w_in = sa("w_in", [128, 512])
            w_cv = sa("w_cv", [128, 2, 4])
            w_cb = sa("w_cb", [128, 2])
            w_xp = sa("w_xp", [128, 2, 33])
            w_dt = sa("w_dt", [33, 256])
            w_db = sa("w_db", [128, 2])
            w_al = sa("w_al", [128, 2, 16])
            w_D = sa("w_D", [128, 2])
            w_out = sa("w_out", [128, 2, 128])
            Am = sa("Am", [128, 32])
            f_w1 = sa("f_w1", [128, 9, 512])
            f_w2 = sa("f_w2", [128, 9, 4, 128])
            f_g = sa("f_g", [128, 8])
            hl = sa("hl", [128, 32])
            C = 512
            NA, NR, NW, NP = 3, 2, 3, 2
            xn1 = sa("xn1", [128, 4, 128])
            xin = sa("xin", [128, 2, C + 3])
            cv = sa("cv", [128, 2, C])
            row = sa("row", [33, C])
            s16 = sa("s16", [32, C], BF16)
            sr1 = sa("sr1", [32, C])
            vv = sa("vv", [128, C])
            pp_, yy = cv[:, 0, :], cv[:, 1, :]
            sq = xn1[:, :, :].rearrange("p b d -> p (b d)")
            fsq = [None]
            U = [sa(f"U{i}", [128, 2, C]) for i in range(3)]
            ZS = [sa(f"ZS{i}", [128, 2, C]) for i in range(2)]
            DL = [sa(f"DL{i}", [128, 2, C]) for i in range(2)]
            DU = [sa(f"DU{i}", [128, 2, C]) for i in range(2)]
            S3 = [sa(f"S3{i}", [96, C], BF16) for i in range(2)]
            ab = [sa(f"ab{i}", [128, 2, C])[:, :, :] for i in range(NA)]
            rb = [sa(f"rb{i}", [128, 2, C])[:, :, :] for i in range(NR)]
            wb = [sa(f"wb{i}", [128, 2, C])[:, :, :] for i in range(NW)]
            pb = [sa(f"pb{i}", [128, 2, C])[:, :, :] for i in range(NP)]
            Bb = [sa(f"Bb{i}", [128, C])[:, :] for i in range(3)]
            Cb = [sa(f"Cb{i}", [128, C])[:, :] for i in range(3)]
            TH = [sa(f"TH{i}", [128, C])[:, :] for i in range(3)]
            HB = [sa(f"HB{i}", [128, C])[:, :] for i in range(8)]
            xn2 = sa("xn2", [128, 4, 128])
            lg = sa("lg", [128, 4, 8])
            oh = sa("oh", [128, 4, 8])
            tmp = sa("tmp", [128, 4, 8])
            rank = sa("rank", [128, 4, 8])
            G = sa("G", [128, 4, 8])
            mx = sa("mx", [128, 4, 4])

            d_a.start(sp, w_in[:, :], A["L0_attn_in_proj_w"])
            d_a.start(sp, w_cv[:, :, :], A["L0_attn_conv_w"].rearrange("(g p) o k -> p g (o k)", p=128))
            d_a.start(sp, w_cb[:, :], A["L0_attn_conv_b"])
            d_a.start(sp, w_xp[:, :, :], A["L0_attn_x_proj_w"].rearrange("(g p) n -> p g n", p=128))
            d_a.start(sp, w_dt[32:33, :], A["L0_attn_dt_w"])
            d_a.start(sp, w_db[:, :], A["L0_attn_dt_b"])
            d_a.start(sp, w_al[:, :, :], A["L0_attn_A_log"].rearrange("(g p) n -> p g n", p=128))
            d_a.start(sp, w_D[:, :], A["L0_attn_D_param"])
            d_a.start(sp, w_out[:, :, :], A["L0_attn_out_proj_w"].rearrange("(g p) n -> p g n", p=128))
            d_f.start(sp, f_g[:, :], A["L0_ffn_gate_w"])
            d_f.start(sp, f_w1[:, 0, :], A["L0_ffn_shared_w1"])
            d_f.start(sp, f_w1[:, 1:9, :], A["L0_ffn_experts_w1"].rearrange("e d h -> d e h"))
            d_f.start(sp, f_w2[:, 0, :, :], A["L0_ffn_shared_w2"].rearrange("(k p) d -> p k d", p=128))
            for x in range(8):
                d_f.start(sp, f_w2[:, 1 + x, :, :], A["L0_ffn_experts_w2"][x].rearrange("(k p) d -> p k d", p=128))
            wa, wf = d_a.mark(), d_f.mark()
            load_weights()

            for w in (w_cv[:, :, :].rearrange("p g k -> p (g k)"), w_cb[:, :]):
                mw = dve.do(lambda e, w=w: e.tensor_scalar(w, w, 0.5, None, ALU.mult), wa)
            z0 = dve.do(lambda e: e.memset(xin[:, :, 0:3], 0.0))
            mA = act.do(lambda e: e.activation(Am[:, :], w_al[:, :, :].rearrange("p g n -> p (g n)"), ACT.Exp), wa)
            mA = act.do(lambda e: e.mul(Am[:, :], Am[:, :], -1.0), mA)

            b7 = [None]
            P = {}

            def norm(tc, xn, st, mark, bk, bfree_, free_xn):
                b0 = 4 * tc
                for b in range(4):
                    m = dve.do(lambda e, b=b: e.bn_stats(st6[:, st + b, :], x_tok[:, b0 + b, :]), mark)
                yield
                for b in range(4):
                    m2 = dve.do(lambda e, b=b: e.bn_aggr(mv[:, st + b, :], st6[:, st + b, :]), m)
                m = dve.do(lambda e: e.tensor_scalar(rstd[:, st:st + 4], mv[:, st:st + 4, 1], 1e-5, None, ALU.add), m2)
                m = pool.do(lambda e: e.tensor_tensor(rstd[:, st:st + 4], rstd[:, st:st + 4], mhalf[:, 0:4], ALU.pow),
                            m, c2)
                yield
                yield
                for b in range(4):
                    n = dve.do(lambda e, b=b: e.tensor_scalar(xn[:, b, :], x_tok[:, b0 + b, :],
                                                              mv[:, st + b, 0:1], rstd[:, st + b:st + b + 1],
                                                              ALU.subtract, ALU.mult), m, free_xn)
                yield
                for b in range(4):
                    t = pe.do(lambda e, b=b: e.transpose(bank(bk)[:, b * 128:(b + 1) * 128], xn[:, b, :],
                                                         ident[:, :]), n, bfree_[0], c1)
                m = act.do(lambda e: e.activation(XN[:, 512 * tc:512 * tc + 512], bank(bk), ACT.Copy), t)
                bfree_[0] = m
                yield
                return m, t

            pm = dict(s16=None, cv=None, xin=None, row=None, vv=None, yy=None, pp=None, sr=None, xn=None)

            def prolog(tc):
                ts = slice(512 * tc, 512 * tc + 512)
                Ux, Zx, Dx, Vx, Sx = U[tc % 3], ZS[tc % 2], DL[tc % 2], DU[tc % 2], S3[tc % 2]
                ln, pm["xn"] = yield from norm(tc, xn1, 4 * (tc % 2), d_x.mark(), 7, b7, pm["xn"])
                if tc:
                    for g in range(2):
                        z = dve.do(lambda e, g=g: e.tensor_copy(xin[:, g, 0:3], xin[:, g, C:C + 3]), pm["cv"])
                else:
                    z = z0
                mc = []
                for g in range(2):
                    t = mm(bank(7), w_in[:, 128 * g:128 * g + 128], XN[:, ts], True, True, wa, ln, b7[0], sig=True)
                    b7[0] = act.do(lambda e, g=g: e.activation(xin[:, g, 3:3 + C], bank(7), ACT.Copy), t, pm["cv"], z)
                    yield
                    m = dve.do(lambda e, g=g: e.tensor_scalar(cv[:, g, :], xin[:, g, 0:C], w_cv[:, g, 0:1],
                                                              w_cb[:, g:g + 1], ALU.mult, ALU.add),
                               b7[0], z, mw, pm["silu"] if tc else None, pm["pp"])
                    for j in range(1, 4):
                        yield
                        m = dve.do(lambda e, g=g, j=j: e.scalar_tensor_tensor(
                            out=cv[:, g, :], in0=xin[:, g, j:j + C], scalar=w_cv[:, g, j:j + 1], in1=cv[:, g, :],
                            op0=ALU.mult, op1=ALU.add), m)
                    mc.append(m)
                pm["cv"] = m
                yield
                mu = []
                for g in range(2):
                    m = act.do(lambda e, g=g: e.activation(Ux[:, g, :], cv[:, g, :], ACT.Tanh), mc[g],
                               P.get(("u", tc - 3)))
                    yield
                    mu.append(dve.do(lambda e, g=g: e.scalar_tensor_tensor(
                        out=Ux[:, g, :], in0=Ux[:, g, :], scalar=1.0, in1=cv[:, g, :], op0=ALU.add, op1=ALU.mult), m))
                pm["silu"] = mu[-1]
                for g in range(2):
                    t = mm(bank(7), w_in[:, 256 + 128 * g:384 + 128 * g], XN[:, ts], True, True, b7[0], sig=True)
                    m = act.do(lambda e, g=g: e.activation(Zx[:, g, :], bank(7), ACT.Tanh, scale=0.5), t,
                               P.get(("z", tc - 2)))
                    yield
                    b7[0] = dve.do(lambda e, g=g: e.scalar_tensor_tensor(
                        out=Zx[:, g, :], in0=Zx[:, g, :], scalar=1.0, in1=bank(7), op0=ALU.add, op1=ALU.mult), m)
                P["in", tc] = t
                P["mz", tc] = b7[0]
                yield
                for g in range(2):
                    t = mm(bank(7)[0:33, :], w_xp[:, g, :], Ux[:, g, :], g == 0, g == 1, mu[g], b7[0], sig=(g == 1))
                mr = act.do(lambda e: e.activation(row[0:33, :], bank(7)[0:33, :], ACT.Copy), t, pm["row"])
                b7[0] = mr
                yield
                sp3 = [Sx[32 * k:32 * k + 32, :] for k in range(3)]
                m = dve.do(lambda e: e.tensor_copy(sp3[0], row[0:32, :]), mr, P.get(("s", tc - 2)))
                m = dve.do(lambda e: e.tensor_tensor(sr1[:, :], row[0:32, :], sp3[0], ALU.subtract), m)
                yield
                m = dve.do(lambda e: e.tensor_copy(s16[:, :], sr1[:, :]), m, pm["s16"])
                mp = pm["s16"] = act.do(lambda e: e.activation(sp3[1], s16[:, :], ACT.Copy), m, P.get(("s", tc - 2)))
                m = dve.do(lambda e: e.tensor_tensor(sr1[:, :], sr1[:, :], s16[:, :], ALU.subtract), m)
                yield
                m3 = dve.do(lambda e: e.tensor_copy(sp3[2], sr1[:, :]), m)
                P["s3", tc] = [m3, mp]
                P["dl", tc], P["du", tc] = [], []
                for g in range(2):
                    t = mm(bank(7), w_dt[32:33, 128 * g:128 * g + 128], row[32:33, :], True, True, mr, b7[0], sig=True)
                    v1 = act.do(lambda e, g=g: e.activation(vv[:, :], bank(7), ACT.Identity, bias=w_db[:, g:g + 1]),
                                t, pm["vv"])
                    v2 = act.do(lambda e, g=g: e.activation(yy, bank(7), ACT.Abs, bias=w_db[:, g:g + 1]), t,
                                pm["yy"], mu)
                    b7[0] = v2
                    v2 = act.do(lambda e: e.activation(yy, yy, ACT.Exp, scale=-1.0), v2)
                    yield
                    m = dve.do(lambda e: e.tensor_scalar(pp_, yy, LEAD, None, ALU.mult), v2, pm["pp"], mu)
                    for i, (_, im) in enumerate(PAIRS):
                        mq = act.do(lambda e, i=i: e.activation(sq, yy, ACT.Square, bias=cst[:, i:i + 1]), v2,
                                    fsq[0], pm["xn"], c5)
                        yield
                        m = fsq[0] = dve.do(lambda e, i=i, im=im: e.scalar_tensor_tensor(
                            out=pp_, in0=sq, scalar=im * im, in1=pp_, op0=ALU.add, op1=ALU.mult), m, mq)
                        yield
                    pm["yy"] = m
                    m = dve.do(lambda e, g=g: e.scalar_tensor_tensor(out=Dx[:, g, :], in0=vv[:, :], scalar=0.0,
                                                                     in1=pp_, op0=ALU.max, op1=ALU.add), m, v1,
                               P.get(("dlr", tc - 2)))
                    pm["vv"] = pm["pp"] = m
                    P["dl", tc].append(m)
                    P["du", tc].append(pool.do(lambda e, g=g: e.tensor_tensor(Vx[:, g, :], Dx[:, g, :], Ux[:, g, :],
                                                                              ALU.mult), m, mu[g],
                                               P.get(("dur", tc - 2))))
                    yield
                pm["row"] = [t, m3]
                pm["xn"] = [pm["xn"], fsq[0]]

            bc23 = [None, None]
            fa, fr_, fw, fp, fB, fC = [None] * NA, [None] * NR, [None] * NW, [None] * NP, [None] * 3, [None] * 3
            NS = 64
            Mx = {}
            hm = {}
            yev = [None, None]
            late = []

            def flat(v):
                return v.rearrange("p g c -> p (g c)")

            def rows(k):
                tc, n = divmod(k, 16)
                t = mm(bank(2), sel[:, n, :], S3[tc % 2][:, :], True, True, bc23[0], c_sel, P["s3", tc], sig=True)
                bc23[0] = Mx["B", k] = act.do(lambda e: e.activation(Bb[k % 3], bank(2), ACT.Copy), t, fB[k % 3])
                t = mm(bank(3), sel[:, 16 + n, :], S3[tc % 2][:, :], True, True, bc23[1], sig=True)
                P["s", tc] = t
                for g in range(2):
                    c = 16 * g + n
                    Mx["a", k] = act.do(lambda e, g=g, c=c: e.activation(
                        ab[k % NA][:, g, :], DL[tc % 2][:, g, :], ACT.Exp, scale=Am[:, c:c + 1]), mA,
                        P["dl", tc][g], fa[k % NA])
                P["dlr", tc] = Mx["a", k]
                bc23[1] = Mx["C", k] = act.do(lambda e: e.activation(Cb[k % 3], bank(3), ACT.Copy), t, fC[k % 3])

            def clamp(k):
                a, r = flat(ab[k % NA]), flat(rb[k % NR])
                m = dve.do(lambda e: e.tensor_scalar(a, a, 1.0, 1e-8, ALU.min, ALU.max), Mx["a", k])
                Mx["a", k] = m
                Mx["r", k] = act.do(lambda e: e.mul(r[:, 0:2 * C:32], a[:, 0:2 * C:32], E20), m, fr_[k % NR], rz)

            def mulB(k):
                tc = k // 16
                m = pool.do(lambda e: e.tensor_tensor(wb[k % NW], DU[tc % 2][:, :, :],
                                                      Bb[k % 3].unsqueeze(1).to_broadcast([128, 2, C]), ALU.mult),
                            Mx["B", k], fw[k % NW], P["du", tc])
                Mx["w", k] = fB[k % 3] = P["dur", tc] = m

            def scanP(k):
                a, r, p = flat(ab[k % NA]), flat(rb[k % NR]), flat(pb[k % NP])
                Mx["p", k] = dve.do(lambda e: e.tensor_tensor_scan(out=p, data0=a, data1=r, initial=0.0, op0=ALU.mult,
                                                                   op1=ALU.max), Mx["a", k], Mx["r", k], fp[k % NP])
                fr_[k % NR] = Mx["p", k]

            def mulW(k):
                w, p = flat(wb[k % NW]), flat(pb[k % NP])
                Mx["w", k] = dve.do(lambda e: e.scalar_tensor_tensor(out=w, in0=p, scalar=1.0, in1=w, op0=ALU.min,
                                                                     op1=ALU.mult), Mx["p", k], Mx["w", k])

            def scanX(k, g):
                tc, n = divmod(k, 16)
                a, w, p = (v[:, g, :] for v in (ab[k % NA], wb[k % NW], pb[k % NP]))
                init = hl[:, 16 * g + n:16 * g + n + 1] if tc else 0.0
                m = dve.do(lambda e: e.tensor_tensor_scan(out=p, data0=a, data1=w, initial=init, op0=ALU.mult,
                                                          op1=ALU.add), Mx["w", k], hm.get(n))
                fa[k % NA] = Mx["x", k] = m

            def mulC(k):
                tc, n = divmod(k, 16)
                w, p = wb[k % NW], pb[k % NP]
                m = pool.do(lambda e: e.tensor_tensor(w, p, Cb[k % 3].unsqueeze(1).to_broadcast([128, 2, C]),
                                                      ALU.mult), Mx["x", k], Mx["C", k])
                Mx["c", k] = fC[k % 3] = fp[k % NP] = m
                if tc < 3:
                    hm[n] = fp[k % NP] = pool.do(lambda e: e.tensor_copy(
                        hl[:, :].rearrange("p (g n) -> p g n", g=2)[:, :, n:n + 1], p[:, :, C - 1:C]), Mx["x", k])

            def sums(k):
                tc, n = divmod(k, 16)
                for g in range(2):
                    t = mm(bank(g), ident[:, :], wb[k % NW][:, g, :], n == 0, n == 15, Mx["c", k], yev[g], sig=True)
                    if n == 15:
                        late.append((tc, g, t))
                fw[k % NW] = t

            def collect():
                while late:
                    tc, g, t = late.pop(0)
                    Ux = U[tc % 3]
                    m = dve.do(lambda e, g=g, Ux=Ux: e.scalar_tensor_tensor(
                        out=Ux[:, g, :], in0=Ux[:, g, :], scalar=w_D[:, g:g + 1], in1=bank(g), op0=ALU.mult,
                        op1=ALU.add), t, P["du", tc][g])
                    yev[g] = P["y", tc, g] = m

            def epilog(tc):
                Ux, Zx = U[tc % 3], ZS[tc % 2]
                for g in range(2):
                    m = dve.do(lambda e, g=g: e.scalar_tensor_tensor(out=Ux[:, g, :], in0=Ux[:, g, :], scalar=0.5,
                                                                     in1=Zx[:, g, :], op0=ALU.mult, op1=ALU.mult),
                               P["y", tc, g], P["mz", tc])
                P["z", tc] = m
                yield
                for j in range(4):
                    tb = slice(128 * j, 128 * j + 128)
                    for g in range(2):
                        t = mm(bank(6)[:, 128 * j:128 * j + 128], Ux[:, g, tb], w_out[:, g, :], g == 0, g == 1,
                               m, f6[0], sig=True)
                P["u", tc] = t
                yield
                yield
                yield
                xs = x_tok[:, 4 * tc:4 * tc + 4, :].rearrange("p b d -> p (b d)")
                m = dve.do(lambda e: e.tensor_tensor(xs, xs, bank(6), ALU.add), t)
                f6[0] = m
                yield
                ln, em["xn"] = yield from norm(tc, xn2, 8 + 4 * (tc % 2), [m, P["in", tc]], 6, f6, em["xn"])
                em["ln"] = ln
                for b in range(4):
                    t = mm(bank(6)[:, 8 * b:8 * b + 8], XN[:, 512 * tc + 128 * b:512 * tc + 128 * b + 128], f_g[:, :],
                           True, True, wf, ln, sig=True)
                yield
                f6[0] = dve.do(lambda e: e.tensor_copy(lg[:, :, :].rearrange("p b x -> p (b x)"), bank(6)[:, 0:32]), t)
                yield

            def gates(tc):
                m = f6[0]

                def bc(v):
                    return v.unsqueeze(2).to_broadcast([128, 4, 8])

                def first_max(src, mv_, onehot, m):
                    m = dve.do(lambda e: e.tensor_reduce(mv_, src, AX.X, ALU.max), m)
                    m = dve.do(lambda e: e.tensor_tensor(tmp[:, :, :], src, bc(mv_), ALU.is_equal), m)
                    yield
                    m = dve.do(lambda e: e.tensor_tensor(tmp[:, :, :], tmp[:, :, :], rank[:, :, :], ALU.mult), m, rk)
                    m = dve.do(lambda e: e.tensor_reduce(mx[:, 2, :], tmp[:, :, :], AX.X, ALU.max), m)
                    yield
                    return dve.do(lambda e: e.tensor_tensor(onehot, tmp[:, :, :], bc(mx[:, 2, :]), ALU.is_equal), m)

                m = yield from first_max(lg[:, :, :], mx[:, 0, :], oh[:, :, :], m)
                m = dve.do(lambda e: e.scalar_tensor_tensor(out=lg[:, :, :], in0=oh[:, :, :], scalar=-3.0e38,
                                                            in1=lg[:, :, :], op0=ALU.mult, op1=ALU.add), m)
                m = yield from first_max(lg[:, :, :], mx[:, 1, :], G[:, :, :], [m, em["G"]] if em["G"] else m)
                m = dve.do(lambda e: e.tensor_tensor(mx[:, 2, :], mx[:, 1, :], mx[:, 0, :], ALU.subtract), m)
                yield
                m = act.do(lambda e: e.activation(mx[:, 2, :], mx[:, 2, :], ACT.Exp), m)
                yield
                m = dve.do(lambda e: e.tensor_scalar(mx[:, 3, :], mx[:, 2, :], 2.0, 2.0, ALU.mult, ALU.add), m)
                m = dve.do(lambda e: e.reciprocal(mx[:, 3, :], mx[:, 3, :]), m)
                m = dve.do(lambda e: e.tensor_tensor(mx[:, 2, :], mx[:, 2, :], mx[:, 3, :], ALU.mult), m)
                yield
                m = dve.do(lambda e: e.tensor_tensor(oh[:, :, :], oh[:, :, :], bc(mx[:, 3, :]), ALU.mult), m)
                m = dve.do(lambda e: e.tensor_tensor(G[:, :, :], G[:, :, :], bc(mx[:, 2, :]), ALU.mult), m)
                m = dve.do(lambda e: e.tensor_tensor(G[:, :, :], G[:, :, :], oh[:, :, :], ALU.add), m)
                yield
                em["gate"] = m
                yield

            def both(a, b):
                while next(a, 0) is None:
                    yield
                    next(b)
                    yield
                yield from b

            f6 = [None]
            fu = [None, None]
            fh, ft = [None] * 8, [None] * 3
            em = dict(xn=None, G=None)

            def ffn(tc):
                ts = slice(512 * tc, 512 * tc + 512)
                i = 36 * tc
                for e_ in range(9):
                    for j in range(4):
                        k, tk, hk = i % 2, i % 3, i % 8
                        t = mm(bank(4 + k), f_w1[:, e_, 128 * j:128 * j + 128], XN[:, ts], True, True, fu[k], wf,
                               em["ln"], sig=True)
                        m = act.do(lambda e, k=k, tk=tk: e.activation(TH[tk], bank(4 + k), ACT.Tanh, scale=0.5), t,
                                   ft[tk])
                        pend.append((hk, e_, j, tk, k, m))
                        i += 1
                        if len(pend) > 1:
                            hide()
                        if e_:
                            down(tc, (0, 2, 1, 1)[j])
                        yield
                hide()
                for n in (0, 2, 1, 1, 0):
                    down(tc, n)
                    yield
                em["G"] = P["x", tc] = f6[0]

            pend, ready = [], []

            def hide():
                hk, e_, j, tk, k, m = pend.pop(0)
                m = dve.do(lambda e: e.scalar_tensor_tensor(out=HB[hk], in0=TH[tk], scalar=1.0, in1=bank(4 + k),
                                                            op0=ALU.add, op1=ALU.mult), m, fh[hk])
                fu[k] = ft[tk] = m
                ready.append((hk, e_, j, m))

            def down(tc, n):
                if n == 0 and tail:
                    e_, t = tail.pop(0)
                    for b in range(4):
                        xs = x_tok[:, 4 * tc + b, :]
                        f6[0] = xm[b] = dve.do(lambda e, b=b, xs=xs: e.scalar_tensor_tensor(
                            out=xs, in0=bank(6)[:, 128 * b:128 * b + 128],
                            scalar=G[:, b, e_ - 1:e_] if e_ else 0.5, in1=xs, op0=ALU.mult, op1=ALU.add),
                            t, em["gate"], xm[b])
                for _ in range(n):
                    b = nb[0]
                    nb[0] = (b + 1) % 4
                    for i, (hk, e_, j, m) in enumerate(ready[:4]):
                        t = mm(bank(6)[:, 128 * b:128 * b + 128], HB[hk][:, 128 * b:128 * b + 128], f_w2[:, e_, j, :],
                               i == 0, i == 3, m, f6[0], wf, sig=(i == 3))
                    if b == 3:
                        for hk, *_ in ready[:4]:
                            fh[hk] = t
                        del ready[:4]
                        tail.append((e_, t))

            tail = []
            nb = [0]
            xm = [None] * 4

            def drain(gen):
                for _ in gen:
                    pass

            def pull(gen):
                if gen is not None:
                    next(gen, None)

            def SCH(r):
                return 5 if 2 <= r < 8 else 4

            first = prolog(0)
            next(first)
            next(first)
            s0 = pool.do(lambda e: e.memset(sel[:, :, :], 0.0))
            for k in range(3):
                s0 = pool.do(lambda e, k=k: e.affine_select(
                    out=sel[:, :, :], in_=sel[:, :, :], compare_op=ALU.not_equal, fill=1.0,
                    base=-32 * k, pattern=[[-1, 32], [0, 128]], channel_multiplier=1), s0)
            c_sel = s0
            rz = None
            for i in range(NR):
                rz = pool.do(lambda e, i=i: e.memset(rb[i], 0.0))
            rk = None
            for x in range(8):
                rk = pool.do(lambda e, x=x: e.memset(rank[:, :, x], 8.0 - x))
            drain(first)
            sgen = None
            pgen = None
            owed = 0
            for k in range(-2, NS + 1):
                if k >= 0 and k % 16 == 0 and k // 16 < 3:
                    pgen = prolog(k // 16 + 1)
                if k % 16 == 2 and k > 16:
                    if sgen is not None:
                        drain(sgen)
                    tc = k // 16 - 1
                    sgen = iter_chain(epilog(tc), both(gates(tc), ffn(tc)))
                n = SCH(k % 16)
                if k + 2 < NS:
                    rows(k + 2)
                if 0 <= k < NS:
                    mulW(k)
                pull(pgen)
                pull(sgen)
                if n > 3:
                    pull(sgen)
                if 0 <= k + 1 < NS:
                    mulB(k + 1)
                pull(pgen)
                if n > 4:
                    pull(sgen)
                if 0 <= k < NS:
                    scanX(k, 0)
                if n > 5:
                    pull(sgen)
                if 0 <= k + 1 < NS:
                    scanP(k + 1)
                pull(pgen)
                pull(sgen)
                if 0 <= k < NS:
                    scanX(k, 1)
                    mulC(k)
                if k + 2 < NS:
                    clamp(k + 2)
                pull(pgen)
                pull(sgen)
                collect()
                if 0 <= k - 1 < NS:
                    sums(k - 1)
                if k % 16 == 13 and pgen is not None:
                    drain(pgen)
                    pgen = None
            if sgen is not None:
                drain(sgen)
            def later():
                for tc in range(3):
                    _, pm["xn"] = yield from norm(tc, xn1, 4 * (tc % 2), P["x", tc], 7, b7, pm["xn"])

            collect()
            def combine():
                for i, (cn, pn) in enumerate((("convq", "qproj"), ("convk", "kproj"))):
                    for j in range(3):
                        t = mm(bank(7)[:, 128 * j:128 * j + 128], W[cn][:, j, :], W[pn][:, 1, :], True, True, b7[0],
                               d_w.mark(), sig=True)
                    yield
                    m = act.do(lambda e, cn=cn: e.activation(W[cn][:, :, :].rearrange("p j n -> p (j n)"),
                                                             bank(7)[:, 0:384], ACT.Copy), t)
                    yield
                    dve.do(lambda e, cn=cn, pn=pn: e.tensor_tensor(W[cn][:, 1, :], W[cn][:, 1, :], W[pn][:, 0, :],
                                                                   ALU.add), m)
                    yield
                    t = mm(bank(7)[:, 0:1], W[pn][:, 1, :], cols[:, 2 + i:3 + i], True, True, m, sig=True)
                    yield
                    b7[0] = dve.do(lambda e, i=i: e.tensor_tensor(cols[:, 4 + i:5 + i], cols[:, 4 + i:5 + i],
                                                                  bank(7)[:, 0:1], ALU.add), t)
                    yield

            lgen = iter_chain(later(), combine())
            for _ in iter_chain(epilog(3), both(gates(3), ffn(3))):
                pull(lgen)
            drain(lgen)
            meet()

        def stage3(ph):
            def sa(name, shape, dt=F32):
                return sb(name, shape, dt, ph)

            ww = d_w.mark()
            tauR = sa("tauR", [128, T])
            va = sa("va", [128, NB, NH, 32])
            QZ = sa("QZ", [128, 2, NH, 512], BF16)
            tmpl = sa("tmpl", [128, NH])
            KS = sa("KS", [128, 8, T], BF16)
            aa = sa("aa", [128, 16416])
            free1 = QZ[:, 1, :, :].rearrange("p a b -> p (a b)")
            free0 = QZ[:, 0, :, :].rearrange("p a b -> p (a b)").bitcast(F32)
            kp = [free1[:, T * k:T * k + T] for k in range(3)]
            delT = aa[0:16, 0:2048]
            dpart = [aa[0:16, 2048:3072].bitcast(BF16), aa[0:16, 3072:4096].bitcast(BF16), free1[0:16, 3 * T:4 * T]]
            qp = aa[:, 4096:7168].bitcast(BF16).rearrange("p (k t) -> p k t", k=3)
            sc = scratch("sc", [7, 128, T], BF16)
            h_b1 = sa("h_b1", [128, 8, 4])
            h_b2 = sa("h_b2", [8, 128])
            kk = sa("kk", [128, 4, 16])
            c16 = sa("c16", [128, 4, 16])
            sv = sa("sv", [128, 4, 4])
            eA = sa("eA", [128, 2, 4, 8])
            Gh = sa("Gh", [128, NB, 8])
            G2 = sa("G2", [128, 4, 8])
            gT = sa("gT", [8, 512])
            xn4 = sa("xn4", [128, 4, 128])
            d_sk, d_sd = loads("d_sk"), loads("d_sd")
            d_sq = [loads(f"d_sq{q}") for q in range(4)]
            d_r = loads("d_r")
            grp = ([0, 1, 0, 1, 2, 0], [0, 0, 1, 1, 0, 2])

            TC = [aa[:, 2048 * i:2048 * i + 2048] for i in range(4)]
            PD = [aa[:, 8192 + 2056 * i:8192 + 2056 * i + T + 2] for i in range(2)]
            C3 = [aa[:, 12304 + 2048 * i:12304 + 2048 * i + 2048] for i in range(2)]
            xn3 = C3[0][:, 0:512].rearrange("p (b d) -> p b d", b=4)
            for b in range(4):
                m = dve.do(lambda e, b=b: e.bn_stats(st6[:, b, :], x_tok[:, 12 + b, :]))
            for b in range(4):
                m2 = dve.do(lambda e, b=b: e.bn_aggr(mv[:, b, :], st6[:, b, :]), m)
            m = dve.do(lambda e: e.tensor_scalar(rstd[:, 0:4], mv[:, 0:4, 1], 1e-5, None, ALU.add), m2)
            m = pool.do(lambda e: e.tensor_tensor(rstd[:, 0:4], rstd[:, 0:4], mhalf[:, 0:4], ALU.pow), m)
            for b in range(4):
                n = dve.do(lambda e, b=b: e.tensor_scalar(xn3[:, b, :], x_tok[:, 12 + b, :], mv[:, b, 0:1],
                                                          rstd[:, b:b + 1], ALU.subtract, ALU.mult), m)
            for b in range(4):
                t = pe.do(lambda e, b=b: e.transpose(bank(0)[:, b * 128:(b + 1) * 128], xn3[:, b, :], ident[:, :]), n)
            ln = [None] * 3 + [act.do(lambda e: e.activation(XN[:, 1536:2048], bank(0), ACT.Copy), t)]
            mxn = (pe.sem, pe.count)
            zp = [pool.do(lambda e, i=i, c=c: e.memset(PD[i][:, c:c + 1], 0.0)) for i in range(2) for c in (0, T + 1)]
            z1 = pool.do(lambda e: e.memset(tmpl[:, :], 1.0))
            for hh in range(2):
                tv = tmpl[:, hh:NH:2]
                z1 = pool.do(lambda e, tv=tv, hh=hh: e.affine_select(
                    out=tv, in_=tv, compare_op=ALU.is_ge, fill=0.0, base=-(64 * hh + 48), pattern=[[0, 8]],
                    channel_multiplier=1), z1)
                z1 = pool.do(lambda e, tv=tv, hh=hh: e.affine_select(
                    out=tv, in_=tv, compare_op=ALU.is_ge, fill=0.0, base=64 * hh + 50, pattern=[[0, 8]],
                    channel_multiplier=-1), z1)
            zrow = sa("zrow", [3, 512], BF16)
            zz = pool.do(lambda e: e.memset(zrow[:, :], 0.0))
            z2 = pool.do(lambda e: e.memset(KS[:, :, :].bitcast(mybir.dt.uint32), 0x3F803F80))
            cm = None
            for x in range(16):
                cm = pool.do(lambda e, x=x: e.memset(kk[:, :, x], float(x + 1)))
            for x in range(8):
                cm = pool.do(lambda e, x=x: e.memset(eA[:, 0, :, x], float(x)))
                cm = pool.do(lambda e, x=x: e.memset(eA[:, 1, :, x], float((x + 7) % 8)))
            zq = pool.do(lambda e: e.memset(va[:, :, :, :], 0.0))
            zq = pool.do(lambda e: e.memset(va[:, :, :, 8:9], 1.0), zq)
            zb = [act.do(lambda e: e.activation(QZ[:, 0, :, :], tmpl[:, :].unsqueeze(2).to_broadcast([128, NH, 512]),
                                                ACT.Copy), z1)]
            free = [None] * 8
            order = (("Wk", "convk", "kproj", 1), ("Wq", "convq", "qproj", 0))
            ev_ = {}
            bk = 0
            for wn, cn, pn, i in order:
                for q in range(4):
                    k = 2 + bk % 4
                    bk += 1
                    t = mm(bank(k), W[wn][:, :], XN[:, 512 * q:512 * q + 512], True, True, free[k], ww, ln[q], sig=True)
                    free[k] = ev_[i, q] = act.do(lambda e, k=k, q=q, i=i: e.activation(
                        PD[i][:, 1 + 512 * q:513 + 512 * q], bank(k), ACT.Identity, bias=cols[:, i:i + 1]), t, ww)
            mcv = {}
            for i in range(2):
                for g in range(2):
                    c = TC[2 * i + g]
                    m = dve.do(lambda e, i=i, g=g, c=c: e.tensor_scalar(
                        c, xnT[:, 0:T], t1w[:, i, g, 0:1], t1w[:, i, g, 3:4], ALU.mult, ALU.add), ww, ln[3], mxn)
                    for j in (1, 2):
                        m = dve.do(lambda e, i=i, g=g, j=j, c=c: e.scalar_tensor_tensor(
                            out=c, in0=xnT[:, j:j + T], scalar=t1w[:, i, g, j:j + 1], in1=c,
                            op0=ALU.mult, op1=ALU.add), m)
                    mcv[i, g] = m
            ev3 = {}

            def conv(wn, cn, pn, i):
                nonlocal bk
                for q in range(4):
                    k = 2 + bk % 4
                    bk += 1
                    for j in range(3):
                        t = mm(bank(k), W[cn][:, j, :], PD[i][:, 512 * q + j:512 * q + j + 512], j == 0, j == 2,
                               free[k], ev_[i, q], ev_[i, min(q + 1, 3)], zp[-1], sig=(j == 2))
                    free[k] = ev3[i, q] = act.do(lambda e, k=k, q=q, i=i: e.activation(
                        C3[i][:, 512 * q:512 * q + 512], bank(k), ACT.Identity, bias=cols[:, 4 + i:5 + i]), t, mxn)

            gl, ms = {}, {}

            def gelu(i):
                for g in range(2):
                    gl[i, g] = act.do(lambda e, c=TC[2 * i + g]: e.activation(c, c, ACT.Gelu), mcv[i, g])

            def gate(i, before):
                nonlocal bk
                for q in range(4):
                    s = slice(512 * q, 512 * q + 512)
                    k = 2 + bk % 4
                    bk += 1
                    w2, o, bcol, M = ((t2w, tauR, cols[:, 6:7], 128), (d2w, delT, cols[0:16, 7:8], 16))[i]
                    for g in range(2):
                        t = mm(bank(k)[0:M, :], w2[:, g, :], TC[2 * i + g][:, s], g == 0, g == 1, gl[i, g], free[k],
                               ww, sig=True)
                    free[k] = ms[i, q] = act.do(lambda e, o=o, s=s, k=k, M=M, bcol=bcol: e.activation(
                        o[:, s], bank(k)[0:M, :], ACT.Sigmoid, bias=bcol), t, before)
                return t

            def parts_of(src, outs, *marks):
                m = dve.do(lambda e: e.tensor_copy(outs[0], src), *marks)
                m = dve.do(lambda e: e.tensor_tensor(src, src, outs[0], ALU.subtract), m)
                m = dve.do(lambda e: e.tensor_copy(outs[1], src), m)
                m = dve.do(lambda e: e.tensor_tensor(src, src, outs[1], ALU.subtract), m)
                return dve.do(lambda e: e.tensor_copy(outs[2], src), m)

            d_q = [loads(f"d_q{i}") for i in range(2)]
            used = [None, None]
            qkm = {}
            mqs = []

            def load_q(qc):
                sl = qc % 2
                qs = slice(512 * qc, 512 * qc + 512)
                for hh in range(2):
                    for gi, pk in enumerate(grp[0]):
                        srcd = sc[pk, :, qs].rearrange("(a b r) t -> b r a t", b=2, r=8)[hh]
                        d_q[sl].start(sp, QZ[64 * hh + 8 * gi:64 * hh + 8 * gi + 8, sl, hh:NH:2, :], srcd, mqs[qc], zb[sl],
                                      used[sl])
                    if qc >= 2:
                        d_q[sl].start(sp, QZ[64 * hh + 51:64 * hh + 54, sl, hh:NH:2, :], zrow[:, :].unsqueeze(1).to_broadcast([3, 8, 512]), zz, used[sl])
                qkm[qc] = d_q[sl].mark()

            conv(*order[0])
            gelu(0)
            gelu(1)
            mk = parts_of(C3[1], kp, ev3[1, 3])
            for k in range(3):
                d_sk.start(sp, sc[3 + k, :, :], kp[k], mk)
            mks = d_sk.mark()
            for hh in range(2):
                for gi, pk in enumerate(grp[1]):
                    srcd = sc[3 + pk].rearrange("(a b r) t -> b r a t", b=2, r=8)[hh]
                    d_r.start(sp, KS[64 * hh + 8 * gi:64 * hh + 8 * gi + 8, :, :], srcd, mks, z2)
            ttc = gate(0, None)
            ttd = gate(1, ttc)
            md = parts_of(delT, dpart, ms[1, 3], ttc)
            for k in range(3):
                d_sd.start(sp, sc[6, 16 * k:16 * k + 16, :], dpart[k], md)
            mds = d_sd.mark()
            conv(*order[1])
            tq = (pe.sem, pe.count)
            for q in range(4):
                s = slice(512 * q, 512 * q + 512)
                m = dve.do(lambda e, s=s: e.scalar_tensor_tensor(
                    out=C3[0][:, s], in0=C3[0][:, s], scalar=float(8.0 ** -0.5), in1=tauR[:, s], op0=ALU.mult,
                    op1=ALU.mult), ms[0, q], ev3[0, q])
                m = parts_of(C3[0][:, s], [qp[:, k, s] for k in range(3)], m, ttd)
                for k in range(3):
                    d_sq[q].start(sp, sc[k, :, s], qp[:, k, s], m)
                mqs.append(d_sq[q].mark())
                if q == 0:
                    for hh in range(2):
                        for k in range(3):
                            srcd = sc[6, 16 * k:16 * k + 16, :].rearrange("(a b) t -> b a t", b=2)[hh:hh + 1, :, :]
                            d_r.start(sp, KS[64 * hh + 48 + k:64 * hh + 49 + k, :, :], srcd, mds, z2)
                    mqk = d_r.mark()
                    load_q(0)
            zb.append(act.do(lambda e: e.activation(QZ[:, 1, :, :], tmpl[:, :].unsqueeze(2).to_broadcast(
                [128, NH, 512]), ACT.Copy), z1, mks, mds))
            for q in range(4):
                k = 2 + q
                for b in range(4):
                    tb = 4 * q + b
                    t = mm(bank(k)[:, 128 * b:128 * b + 128], XN[:, 128 * tb:128 * tb + 128], W["Wv"][:, :],
                           True, True, free[k], sig=True)
                for b in range(4):
                    tb = 4 * q + b
                    m = dve.do(lambda e, k=k, b=b, tb=tb: e.tensor_tensor(
                        va[:, tb, :, 0:8], bank(k)[:, 128 * b:128 * b + 128].rearrange("p (h r) -> p h r", h=16),
                        bb[:, 0, :].rearrange("p (h r) -> p h r", h=16), ALU.add), t, zq)
                free[k] = m
            mva = m
            NG = 16
            Pt = [aa[:, 2048 * i:2048 * i + 2048] for i in range(3)]
            Oe = aa[:, 6144:6656]
            nm = aa[0:4, 6656:7168]
            n1, n2 = aa[0:4, 7168:7680], aa[0:4, 7680:8192]
            n3 = aa[0:4, 8192:8960].bitcast(BF16).rearrange("p (k t) -> p k t", k=3)
            rs = aa[:, 8960:8976]
            mx4 = aa[:, 9024:9024 + 64].rearrange("p (b h c) -> p b h c", b=4, h=4)
            mxh = aa[:, 9088:9104].rearrange("p (b h) -> p b h", b=4)
            at = aa[:, 9216:9728].rearrange("p (b d) -> p b d", b=4)
            att = aa[:, 9728:10240]
            fS = [None] * 3
            fP = [mqs + [mds, mks, tq]] * 3
            fM = [None] * 3
            cs = 0
            fO = [None, None]
            xr, gr, xb = {}, {}, {}
            d_g = loads("d_g")
            d_h = loads("d_h")
            d_h.start(sp, h_b1[:, :, :], A["L1_ffn_b1"])
            d_h.start(sp, h_b2[:, :], A["L1_ffn_b2"])
            wb2 = d_h.mark()
            hw1 = [aa[:, 10240 + 512 * x:10752 + 512 * x] for x in range(8)]
            hw2 = ([aa[:, 14336 + 512 * x:14848 + 512 * x] for x in range(4)]
                   + [tauR[:, 512 * x:512 * x + 512] for x in range(4)])
            stt = dict(xn4=None, gT=None, n3=mqs + [tq], mxh=None, nm=tq, at=tq, att=tq, oe=mqs, last=None)
            d_n = loads("d_n")
            d_m = loads("d_m")
            mrow = {}

            def first_maxima():
                buf = [aa[:, 512 * i:512 * i + 512] for i in range(8)]
                fb, fk = [[mds, mks, tq]] * 8, [ln[3], None] + free[2:6]
                cnt = 0
                for b in range(4):
                    for h in range(4):
                        m = None
                        for c in range(4):
                            k, i = cnt % 6, (cnt // 2) % 8
                            cnt += 1
                            t = mm(bank(k), QZ[:, 0, h, 128 * b:128 * b + 128], KS[:, h // 2, 512 * c:512 * c + 512],
                                   True, True, fk[k], mqk, qkm[0], sig=True)
                            if c % 2 == 0:
                                fk[k] = ma = act.do(lambda e, k=k, i=i: e.activation(buf[i], bank(k), ACT.Copy), t,
                                                    fb[i])
                            else:
                                init = buf[(i - 1) % 8][:, 511:512] if c == 3 else -3.0e38
                                fk[k] = m = dve.do(lambda e, k=k, i=i, init=init: e.tensor_tensor_scan(
                                    out=buf[i], data0=bank(k), data1=buf[i], initial=init, op0=ALU.max, op1=ALU.max),
                                    t, ma, m)
                        m = dve.do(lambda e, b=b, h=h, i=i: e.tensor_scalar(mxh[:, b, h:h + 1], buf[i][:, 511:512],
                                                                           -1.0, None, ALU.mult), m)
                        fb[i] = fb[(i - 1) % 8] = m
                fS[:] = fk[0:3]
                fM[:] = fk[3:6]
                fP[:] = [m] * 3
                yield from finish_maxima(0, m)

            def maxima(G):
                qc, hg = divmod(G, 4)
                cnt = 1
                for b in range(4):
                    for hl_ in range(4):
                        h = 4 * hg + hl_
                        for c in range(4):
                            k = cnt % 3
                            cnt += 1
                            t = mm(bank(3 + k), QZ[:, qc % 2, h, 128 * b:128 * b + 128],
                                   KS[:, h // 2, 512 * c:512 * c + 512], True, True, fM[k], mqk, qkm[qc], sig=True)
                            fM[k] = dve.do(lambda e, b=b, hl_=hl_, c=c, k=k: e.tensor_reduce(
                                mx4[:, b, hl_, c:c + 1], bank(3 + k), AX.X, ALU.max), t, stt["mxh"])
                            yield
                m = dve.do(lambda e: e.tensor_reduce(mxh, mx4, AX.X, ALU.max, negate=True), fM, stt["nm"])
                stt["mxh"] = m
                yield
                yield
                yield from finish_maxima(G, m)

            def finish_maxima(G, m):
                qc, hg = divmod(G, 4)
                for b in range(4):
                    t = pe.do(lambda e, b=b: e.transpose(bank(3)[0:4, 128 * b:128 * b + 128], mxh[:, b, :],
                                                         ident[:, :]), m, fM[0])
                stt["nm"] = t
                m = act.do(lambda e: e.activation(nm, bank(3)[0:4, :], ACT.Copy), t, stt["n3"])
                fM[0] = m
                yield
                lane = pool if G else dve
                m0 = lane.do(lambda e: e.tensor_copy(n3[:, 0, :], nm), m, d_n.mark() if G else None)
                m = lane.do(lambda e: e.tensor_tensor(n1, nm, n3[:, 0, :], ALU.subtract), m0)
                m = lane.do(lambda e: e.tensor_copy(n3[:, 1, :], n1), m)
                m = lane.do(lambda e: e.tensor_tensor(n2, n1, n3[:, 1, :], ALU.subtract), m)
                m = lane.do(lambda e: e.tensor_copy(n3[:, 2, :], n2), m)
                stt["n3"] = m
                qs = slice(512 * qc, 512 * qc + 512)
                nd = sc[6, 48:96, qs].rearrange("(k g h) t -> g h k t", k=3, g=4)[hg]
                d_n.start(sp, nd, n3, m)
                for hh in range(2):
                    srcd = sc[6, 48:96, qs].rearrange("(k g a b) t -> g b k a t", k=3, g=4, b=2)[hg, hh]
                    d_m.start(sp, QZ[64 * hh + 51:64 * hh + 54, qc % 2, 4 * hg + hh:4 * hg + 4:2, :], srcd,
                              d_n.mark(), stt["nm"])
                mrow[G] = d_m.mark()
                yield

            def outputs(G, tl):
                qc, hg = divmod(G, 4)
                ob = bank(6 + G % 2)
                m = dve.do(lambda e: e.tensor_copy(Oe, ob), tl, stt["oe"])
                yield
                for b in range(4):
                    tt = pe.do(lambda e, b=b: e.transpose(ob[:, 128 * b:128 * b + 128], Oe[:, 128 * b:128 * b + 128],
                                                          ident[:, :]), m)
                stt["oe"] = tt
                yield
                v7 = ob.rearrange("p (b h c) -> p b h c", b=4, h=4)
                rv = rs.rearrange("p (b h o) -> p b h o", b=4, h=4)
                m = dve.do(lambda e: e.reciprocal(rv, v7[:, :, :, 8:9]), tt)
                for b in range(4):
                    m2 = dve.do(lambda e, b=b: e.tensor_tensor(
                        at[:, b, 32 * hg:32 * hg + 32].rearrange("p (h r) -> p h r", h=4),
                        v7[:, b, :, 0:8], rv[:, b, :, :].to_broadcast([128, 4, 8]), ALU.mult), m, stt["at"])
                fO[G % 2] = m2
                yield
                if hg == 3:
                    for b in range(4):
                        tt = pe.do(lambda e, b=b: e.transpose(ob[:, 128 * b:128 * b + 128], at[:, b, :],
                                                              ident[:, :]), m2)
                    stt["at"] = tt
                    yield
                    m = act.do(lambda e: e.activation(att, ob, ACT.Copy), tt, stt["att"])
                    yield
                    for b in range(4):
                        t = mm(ob[:, 128 * b:128 * b + 128], att[:, 128 * b:128 * b + 128], W["out"][:, :],
                               True, True, m, sig=True)
                    stt["att"] = t
                    yield
                    xs = x_tok[:, 4 * qc:4 * qc + 4, :]
                    b7 = ob.rearrange("p (b d) -> p b d", b=4)
                    m = dve.do(lambda e: e.tensor_tensor(xs, xs, b7, ALU.add), t)
                    fO[G % 2] = m
                    m = dve.do(lambda e: e.tensor_tensor(xs, xs, bb[:, 1:2, :].to_broadcast([128, 4, 128]), ALU.add),
                               m)
                    yield
                    yield from prepare(qc, G % 2, m)

            def prepare(q, ok, m):
                ob = bank(6 + ok)
                b0, st = 4 * q, 4 * q
                m0 = m
                for b in range(4):
                    m = dve.do(lambda e, b=b: e.bn_stats(st6[:, st + b, :], x_tok[:, b0 + b, :]), m0)
                for b in range(4):
                    m2 = dve.do(lambda e, b=b: e.bn_aggr(mv[:, st + b, :], st6[:, st + b, :]), m)
                m = dve.do(lambda e: e.tensor_scalar(rstd[:, st:st + 4], mv[:, st:st + 4, 1], 1e-5, None, ALU.add), m2)
                m = pool.do(lambda e: e.tensor_tensor(rstd[:, st:st + 4], rstd[:, st:st + 4], mhalf[:, 0:4], ALU.pow),
                            m, c2)
                yield
                for b in range(4):
                    n = dve.do(lambda e, b=b: e.tensor_scalar(xn4[:, b, :], x_tok[:, b0 + b, :],
                                                              mv[:, st + b, 0:1], rstd[:, st + b:st + b + 1],
                                                              ALU.subtract, ALU.mult), m, stt["xn4"])
                yield
                for b in range(4):
                    t = pe.do(lambda e, b=b: e.transpose(ob[:, b * 128:(b + 1) * 128], xn4[:, b, :],
                                                         ident[:, :]), n, fO[ok])
                m = act.do(lambda e: e.activation(XN[:, 512 * q:512 * q + 512], ob, ACT.Copy), t)
                fO[ok] = xr[q] = m
                s_, tr, a_, b_ = (sv[:, i, :] for i in range(4))
                m = dve.do(lambda e: e.tensor_tensor(s_, xn4[:, :, 0], xn4[:, :, 1], ALU.add), n)
                stt["xn4"] = [t, m]

                def count(dst, src, n, m):
                    m = dve.do(lambda e: e.tensor_tensor(c16[:, :, 0:n], src.unsqueeze(2).to_broadcast([128, 4, n]),
                                                         kk[:, :, 0:n], ALU.is_ge), m, cm)
                    return dve.do(lambda e: e.tensor_reduce(dst, c16[:, :, 0:n], AX.X, ALU.add), m)

                m = count(a_, s_, 16, m)
                m = dve.do(lambda e: e.tensor_scalar(s_, s_, -1.0, None, ALU.mult), m)
                yield
                m = count(b_, s_, 16, m)
                m = dve.do(lambda e: e.tensor_tensor(tr, a_, b_, ALU.subtract), m)
                m = dve.do(lambda e: e.tensor_scalar(a_, tr, 16.0, 0.125, ALU.add, ALU.mult), m)
                m = count(b_, a_, 4, m)
                m = dve.do(lambda e: e.scalar_tensor_tensor(out=tr, in0=b_, scalar=-8.0, in1=tr, op0=ALU.mult,
                                                            op1=ALU.add), m)
                m = dve.do(lambda e: e.tensor_scalar(tr, tr, 16.0, None, ALU.add), m)
                yield
                hb_ = tr.unsqueeze(2).to_broadcast([128, 4, 8])
                Gq = Gh[:, b0:b0 + 4, :]
                m = dve.do(lambda e: e.tensor_tensor(Gq, eA[:, 0, :, :], hb_, ALU.is_equal), m)
                m = dve.do(lambda e: e.tensor_tensor(G2[:, :, :], eA[:, 1, :, :], hb_, ALU.is_equal), m)
                m = dve.do(lambda e: e.tensor_tensor(Gq, Gq, G2[:, :, :], ALU.add), m)
                m = dve.do(lambda e: e.tensor_scalar(Gq, Gq, 0.5, None, ALU.mult), m)
                gr[q] = m
                yield
                for b in range(4):
                    t = pe.do(lambda e, b=b: e.transpose(ob[0:8, 128 * b:128 * b + 128], Gh[:, b0 + b, :],
                                                         ident[:, :]), m, fO[ok])
                m = act.do(lambda e: e.activation(gT[:, :], ob[0:8, :], ACT.Copy), t, stt["gT"])
                yield
                for b in range(4):
                    t = mm(ob[:, 128 * b:128 * b + 128], gT[:, 128 * b:128 * b + 128], h_b2[:, :], True, True, m, wb2,
                           sig=True)
                stt["gT"] = t
                yield
                xs = x_tok[:, b0:b0 + 4, :].rearrange("p b d -> p (b d)")
                fO[ok] = dve.do(lambda e: e.tensor_tensor(xs, xs, ob, ALU.add), t)
                xb[q] = fO[ok]
                yield

            def pull(gen, n=1):
                for _ in range(n):
                    if gen is not None and next(gen, 0) == 0:
                        return None
                return gen

            def drain(gen):
                for _ in gen:
                    pass

            def all_maxima():
                for G in range(NG):
                    if G % 4 == 2 and G < 14:
                        load_q(G // 4 + 1)
                    yield from maxima(G) if G else first_maxima()

            d_o = loads("d_o")
            ov = out.rearrange("o (b p) d -> p (o b) d", p=128)
            HB = [free0[:, 512 * x:512 * x + 512] for x in range(8)]
            ub = [3]
            fu = [None] * 4

            def experts():
                units = [(q, e_, j) for q in range(4) for e_ in range(8) for j in range(4)]
                wg = d_g.mark()
                fu[3] = fM[0]
                fh, fd, xm = [used[0]] * 8, [fM[1], fM[2]], [None] * 4
                ready, blocks = [], []

                def block():
                    q, e_, b, hs = blocks.pop(0)
                    k = e_ % 2
                    for i, (hk, m) in enumerate(hs):
                        t = mm(bank(4 + k)[:, 128 * b:128 * b + 128], HB[hk][:, 128 * b:128 * b + 128],
                               hw2[e_][:, 128 * i:128 * i + 128], i == 0, i == 3, m, fd[k], sig=(i == 3))
                    if b < 3:
                        return
                    for hk, _ in hs:
                        fh[hk] = t
                    for b in range(4):
                        xs = x_tok[:, 4 * q + b, :]
                        m = dve.do(lambda e, b=b, xs=xs: e.scalar_tensor_tensor(
                            out=xs, in0=bank(4 + k)[:, 128 * b:128 * b + 128], scalar=Gh[:, 4 * q + b, e_:e_ + 1],
                            in1=xs, op0=ALU.mult, op1=ALU.add), t, gr[q], xb[q], xm[b])
                        xm[b] = m
                    fd[k] = m
                    if e_ == 7:
                        d_o.start(sp, ov[:, 4 * q:4 * q + 4, :], x_tok[:, 4 * q:4 * q + 4, :], m)

                for i, (q, e_, j) in enumerate(units):
                    k, hk = ub[i % len(ub)], i % 8
                    t = mm(bank(k), hw1[e_][:, 128 * j:128 * j + 128], XN[:, 512 * q:512 * q + 512], True, True,
                           fu[k], wg, xr[q], sig=True)
                    fu[k] = m = act.do(lambda e, k=k, hk=hk, e_=e_, j=j: e.activation(
                        HB[hk], bank(k), ACT.Relu, bias=h_b1[:, e_, j:j + 1]), t, fh[hk], wb2)
                    ready.append((hk, m))
                    if blocks:
                        block()
                    if j == 3:
                        blocks += [(q, e_, b, ready[:]) for b in range(4)]
                        del ready[:]
                    yield
                while blocks:
                    block()
                yield

            gen = all_maxima()
            xg = None
            gen = pull(gen, 3 + LEAD_PULLS)
            post = None
            for G in range(NG):
                qc, hg = divmod(G, 4)
                if 1 <= G <= 8:
                    d_g.start(sp, hw1[G - 1], A["L1_ffn_W1"][G - 1])
                    d_g.start(sp, hw2[G - 1].rearrange("p (k d) -> p k d", k=4),
                              A["L1_ffn_W2"][G - 1].rearrange("(k p) d -> p k d", p=128))

                def pv(kb, pt, ms):
                    for j in range(4):
                        f = pe.do if j == 3 else pe.quiet
                        t = f(lambda e, j=j, kb=kb, pt=pt, hg=hg, G=G: e.matmul(
                            bank(6 + G % 2)[32 * j:32 * j + 32, :], va[:, kb, 4 * hg + j, :],
                            pt[:, 512 * j:512 * j + 512], start=(kb == 0), stop=(kb == NB - 1)),
                            ms, fO[G % 2] if kb == 0 else None, mva)
                    return t

                pend = None
                for kb in range(NB):
                    pt = Pt[kb % 3]
                    ms = []
                    for n in range(4):
                        h, sk = 4 * hg + n, cs % 3
                        cs += 1
                        t = mm(bank(sk), KS[:, h // 2, 128 * kb:128 * kb + 128], QZ[:, qc % 2, h, :], True, True,
                               fS[sk], mrow[G], sig=True)
                        fS[sk] = act.do(lambda e, pt=pt, n=n, sk=sk: e.activation(
                            pt[:, 512 * n:512 * n + 512], bank(sk), ACT.Exp), t, fP[kb % 3])
                        ms.append(fS[sk])
                        gen = pull(gen, 1 + (n == 3 and kb % 4 == 1))
                        if gen is None and n == 3:
                            xg = pull(xg or experts())
                        if n == 1 and pend is not None:
                            fP[(kb - 1) % 3] = pv(*pend)
                    pend = (kb, pt, ms)
                    if kb >= 1:
                        post = pull(post)
                fP[(NB - 1) % 3] = tl = pv(*pend)
                while post is not None and hg != 0:
                    post = pull(post)
                used[qc % 2] = tl
                if post is not None:
                    drain(post)
                post = outputs(G, tl)
            ub[:] = [0, 1, 2, 3]
            fu[0:3] = fS
            while post is not None or xg is not None:
                post = pull(post)
                xg = pull(xg)
            sp.wait(d_o.mark())

        for stage in (stage1, stage3):
            with ExitStack() as ph:
                stage(ph)
        play(ctx, nc, lanes)


def play(ctx, nc, lanes):
    pe, act, dve, pool, sp = lanes
    block = ctx.enter_context(nc.Block())

    @block.tensor
    def _(e):
        pe.play(e)

    @block.scalar
    def _(e):
        act.play(e)

    @block.vector
    def _(e):
        dve.play(e)

    @block.gpsimd
    def _(e):
        pool.play(e)

    @block.sync
    def _(e):
        sp.play(e)


def kernel(**inputs):
    import numpy as _np
    import concourse.bacc as _bacc
    from concourse import mybir as _mybir
    from concourse.bass_utils import run_bass_kernel_spmd as _run

    a = {k: _np.asarray(v) for k, v in inputs.items()}
    lay = dict(a)
    for n in ("L0_attn_conv_b", "L0_attn_dt_b", "L0_attn_D_param"):
        lay[n] = a[n].reshape(2, 128).T
    lay["L0_ffn_shared_w1"] = a["L0_ffn_shared_w1"].T
    lay["L0_ffn_shared_w2"] = a["L0_ffn_shared_w2"].T
    lay["L0_ffn_experts_w1"] = a["L0_ffn_experts_w1"].transpose(0, 2, 1)
    lay["L0_ffn_experts_w2"] = a["L0_ffn_experts_w2"].transpose(0, 2, 1)
    lay["L0_ffn_gate_w"] = a["L0_ffn_gate_w"].T
    for n in ("Wq_w", "Wk_w", "Wv_w", "out_w", "qproj_w", "kproj_w"):
        lay["L1_attn_" + n] = a["L1_attn_" + n].T
    for n in ("convq_w", "convk_w"):
        lay["L1_attn_" + n] = a["L1_attn_" + n].transpose(0, 2, 1)
    rep = _np.repeat(a["L1_attn_tau2_b"], 8)
    lay["cols"] = _np.stack([lay.pop("L1_attn_" + n) for n in ("Wq_b", "Wk_b", "convq_b", "convk_b", "qproj_b",
                                                              "kproj_b")]
                            + [rep, _np.pad(lay.pop("L1_attn_del2_b"), (0, 112))], axis=1)
    lay.pop("L1_attn_tau2_b")
    lay["t1w"] = _np.stack([_np.concatenate([lay.pop(f"L1_attn_{n}_w").reshape(128, 2, 3),
                                             lay.pop(f"L1_attn_{n}_b").reshape(128, 2, 1)], axis=2)
                            for n in ("tau1", "del1")], axis=1)
    lay["L1_attn_tau2_w"] = _np.repeat(a["L1_attn_tau2_w"][:, :, 0], 8, axis=0).T
    lay["L1_attn_del2_w"] = a["L1_attn_del2_w"][:, :, 0].T
    lay["L1_ffn_b1"] = a["L1_ffn_b1"].reshape(8, 4, 128).transpose(2, 0, 1)
    nc = _bacc.Bacc("TRN2", target_bir_lowering=False, num_devices=1)
    arrays, aps = {}, {}
    for n, v in lay.items():
        v = _np.ascontiguousarray(v)
        arrays[f"in_{n}"] = v
        aps[n] = nc.dram_tensor(f"in_{n}", v.shape, _mybir.dt.from_np(v.dtype), kind="ExternalInput").ap()
    o = nc.dram_tensor("out_0", (1, 2048, 128), _mybir.dt.float32, kind="ExternalOutput").ap()
    build(nc, aps, o)
    r = _run(nc, [arrays], core_ids=[0])
    return r.results[0]["out_0"]
```
